# Optimizing a Trainium2 kernel written in Bass

```python
import numpy as np
import jax
import jax.numpy as jnp

def _softmax(x, axis=-1):
    return jax.nn.softmax(x, axis=axis)

def _gelu(x):
    return jax.nn.gelu(x, approximate=True)

def _silu(x):
    return jax.nn.silu(x)

def _sigmoid(x):
    return jax.nn.sigmoid(x)

def _layernorm(x, axis=-1, eps=1e-05):
    m = jnp.mean(x, axis=axis, keepdims=True)
    v = jnp.var(x, axis=axis, keepdims=True)
    return (x - m) / jnp.sqrt(v + eps)

def _scatter_add(tgt, idx, src, axis=0):
    return tgt.at[idx].add(src)

def _segment_sum(src, seg, n):
    return jax.ops.segment_sum(src, seg, n)
kernel_name = 'mk_adj_resnorm_d4_adj_r2_60d617'

def setup_inputs(seed: int=0):
    np.random.seed(seed)
    _w = jnp.asarray

    def _rec_inputs():
        import jax
        import jax.numpy as jnp
        _gk = jax.random.key(seed)
        x = -0.0002928 + 1 * jax.random.normal(jax.random.fold_in(_gk, 1), (4096, 256), jnp.float32)
        _a = jax.random.bernoulli(jax.random.fold_in(_gk, 2), 0.00195312, (4096, 4096))
        _a = jnp.logical_or(_a, jnp.swapaxes(_a, -1, -2))
        _a = jnp.logical_or(_a, jnp.eye(4096, dtype=bool))
        _af = _a.astype(jnp.float32)
        _af = _af / jnp.maximum(_af.sum(-1, keepdims=True), 1.0)
        adj = _af
        return (x, adj)
    x, adj = _rec_inputs()

    def _L0_gnn_setup():
        import jax, jax.numpy as jnp
        import numpy as np
        N = 4096
        D = 256
        H = 256

        def _graph_conv(feats, adj, W, b):
            agg = adj @ feats
            cat = jnp.concatenate([feats, agg], axis=-1)
            return jax.nn.relu(jnp.einsum('nd,df->nf', cat, W) + b)
        key = jax.random.key(seed)
        k1, k2, k3, k4 = jax.random.split(key, 4)
        x = jax.random.normal(k1, (N, D), dtype=jnp.float32)
        adj = jax.random.uniform(k2, (N, N), dtype=jnp.float32)
        adj = adj / jnp.sum(adj, axis=-1, keepdims=True)
        lim1 = float(np.sqrt(6.0 / (2 * D + H)))
        lim2 = float(np.sqrt(6.0 / (2 * H + H)))
        W1 = jax.random.uniform(k3, (2 * D, H), dtype=jnp.float32, minval=-lim1, maxval=lim1)
        W2 = jax.random.uniform(k4, (2 * H, H), dtype=jnp.float32, minval=-lim2, maxval=lim2)
        b1 = jnp.zeros((H,), dtype=jnp.float32)
        b2 = jnp.zeros((H,), dtype=jnp.float32)
        return {'x': x, 'adj': adj, 'W1': W1, 'b1': b1, 'W2': W2, 'b2': b2}
    _L0_gnn_all = _L0_gnn_setup()
    _L0_gnn_in = {k: v for k, v in _L0_gnn_all.items() if k in ('W1', 'b1', 'W2', 'b2')}
    del _L0_gnn_all

    def _L1_gnn_setup():
        import jax, jax.numpy as jnp
        import numpy as np
        N = 4096
        D_IN = 256
        HEADS = 8
        DPH = 256 // HEADS
        EDGE_P = 0.01
        key = jax.random.key(seed)
        k1, k2, k3 = jax.random.split(key, 3)
        H = jax.random.normal(k1, (N, D_IN), dtype=jnp.float32)
        adj = (jax.random.uniform(k2, (N, N)) < EDGE_P).astype(jnp.float32)
        limit = float(np.sqrt(6.0 / (D_IN + DPH)))
        W = jax.random.uniform(k3, (HEADS, D_IN, DPH), jnp.float32, -limit, limit)
        b = jnp.zeros((HEADS, DPH), jnp.float32)
        return {'H': H, 'adj': adj, 'W': W, 'b': b}
    _L1_gnn_all = _L1_gnn_setup()
    _L1_gnn_in = {k: v for k, v in _L1_gnn_all.items() if k in ('W', 'b')}
    del _L1_gnn_all

    def _L2_gnn_setup():
        import jax, jax.numpy as jnp
        import numpy as np
        N, IN_F, OUT_F = (4096, 256, 256)
        HID = OUT_F // 2
        key = jax.random.key(seed)
        ks = jax.random.split(key, 6)
        x = jax.random.normal(ks[0], (N, IN_F), dtype=jnp.float32)
        adj = jax.random.uniform(ks[1], (N, N), dtype=jnp.float32)
        W1 = jax.random.normal(ks[2], (HID, IN_F), dtype=jnp.float32) * np.sqrt(2.0 / IN_F)
        b1 = jnp.zeros((HID,), dtype=jnp.float32)
        W2 = jax.random.normal(ks[3], (OUT_F, HID), dtype=jnp.float32) * np.sqrt(2.0 / HID)
        b2 = jnp.zeros((OUT_F,), dtype=jnp.float32)
        return {'x': x, 'adj': adj, 'W1': W1, 'b1': b1, 'W2': W2, 'b2': b2}
    _L2_gnn_all = _L2_gnn_setup()
    _L2_gnn_in = {k: v for k, v in _L2_gnn_all.items() if k in ('W1', 'b1', 'W2', 'b2')}
    del _L2_gnn_all

    def _L3_gnn_setup():
        import jax, jax.numpy as jnp
        import numpy as np
        EPS = 1e-08
        key = jax.random.key(seed)
        k1, k2, k3, k4 = jax.random.split(key, 4)
        N, IN, OUT = (4096, 256, 256)
        x = jax.random.normal(k1, (N, IN), dtype=jnp.float32)
        adj = jax.random.uniform(k2, (N, N), dtype=jnp.float32)
        W = jax.random.normal(k3, (OUT, IN), dtype=jnp.float32) * (1.0 / np.sqrt(IN))
        b = jax.random.normal(k4, (OUT,), dtype=jnp.float32) * 0.01
        return {'x': x, 'adj': adj, 'W': W, 'b': b}
    _L3_gnn_all = _L3_gnn_setup()
    _L3_gnn_in = {k: v for k, v in _L3_gnn_all.items() if k in ('W', 'b')}
    del _L3_gnn_all
    return {'x': x, 'adj': adj, 'L0_gnn_W1': _L0_gnn_in['W1'], 'L0_gnn_b1': _L0_gnn_in['b1'], 'L0_gnn_W2': _L0_gnn_in['W2'], 'L0_gnn_b2': _L0_gnn_in['b2'], 'L1_gnn_W': _L1_gnn_in['W'], 'L1_gnn_b': _L1_gnn_in['b'], 'L2_gnn_W1': _L2_gnn_in['W1'], 'L2_gnn_b1': _L2_gnn_in['b1'], 'L2_gnn_W2': _L2_gnn_in['W2'], 'L2_gnn_b2': _L2_gnn_in['b2'], 'L3_gnn_W': _L3_gnn_in['W'], 'L3_gnn_b': _L3_gnn_in['b']}

def reference(x, adj, L0_gnn_W1, L0_gnn_b1, L0_gnn_W2, L0_gnn_b2, L1_gnn_W, L1_gnn_b, L2_gnn_W1, L2_gnn_b1, L2_gnn_W2, L2_gnn_b2, L3_gnn_W, L3_gnn_b):
    import jax
    import jax.numpy as jnp

    def _L0_gnn_ref(x, adj, W1, b1, W2, b2):
        import jax, jax.numpy as jnp
        import numpy as np
        N = 4096
        D = 256
        H = 256

        def _graph_conv(feats, adj, W, b):
            agg = adj @ feats
            cat = jnp.concatenate([feats, agg], axis=-1)
            return jax.nn.relu(jnp.einsum('nd,df->nf', cat, W) + b)
        h = _graph_conv(x, adj, W1, b1)
        out = jax.nn.relu(_graph_conv(h, adj, W2, b2) + h)
        return out

    def _L1_gnn_ref(H, adj, W, b):
        import jax, jax.numpy as jnp
        import numpy as np
        N = 4096
        D_IN = 256
        HEADS = 8
        DPH = 256 // HEADS
        EDGE_P = 0.01
        H_ = jnp.einsum('nd,hde->hne', H, W)
        out = jnp.einsum('nm,hme->hne', adj, H_) + b[:, None, :]
        return jnp.transpose(out, (1, 0, 2)).reshape(H.shape[0], HEADS * DPH)

    def _L2_gnn_ref(x, adj, W1, b1, W2, b2):
        import jax, jax.numpy as jnp
        import numpy as np
        N, IN_F, OUT_F = (4096, 256, 256)
        HID = OUT_F // 2
        h = x @ W1.T + b1
        h = h @ W2.T + b2
        A = adj + jnp.eye(adj.shape[0], dtype=adj.dtype)
        rowsum = A.sum(axis=1)
        r_inv_sqrt = jnp.power(rowsum, -0.5)
        r_inv_sqrt = jnp.where(jnp.isinf(r_inv_sqrt), 0.0, r_inv_sqrt)
        A = r_inv_sqrt[:, None] * A * r_inv_sqrt[None, :]
        return A.astype(jnp.float32) @ h.astype(jnp.float32)

    def _L3_gnn_ref(x, adj, W, b):
        import jax, jax.numpy as jnp
        import numpy as np
        EPS = 1e-08
        deg = adj.sum(axis=1)
        dis = (deg + EPS) ** (-0.5)
        a_norm = dis[:, None] * adj * dis[None, :]
        h = a_norm @ x
        return h @ W.T + b
    x = _layernorm(x + _L0_gnn_ref(x, adj, L0_gnn_W1, L0_gnn_b1, L0_gnn_W2, L0_gnn_b2), axis=-1)
    x = _layernorm(x + _L1_gnn_ref(x, adj, L1_gnn_W, L1_gnn_b), axis=-1)
    x = _layernorm(x + _L2_gnn_ref(x, adj, L2_gnn_W1, L2_gnn_b1, L2_gnn_W2, L2_gnn_b2), axis=-1)
    x = _layernorm(x + _L3_gnn_ref(x, adj, L3_gnn_W, L3_gnn_b), axis=-1)
    return x

_drawn_inputs = setup_inputs


def setup_inputs(seed=0):
    import zlib

    import numpy as np

    out = dict(_drawn_inputs(seed))
    spreads = {'L0_gnn_b1': (0.0, 0.1),
     'L0_gnn_b2': (0.0, 0.1),
     'L1_gnn_b': (0.0, 0.1),
     'L2_gnn_b1': (0.0, 0.1),
     'L2_gnn_b2': (0.0, 0.1)}
    factors = {'L3_gnn_b': 6.962}
    for name, (base, spread) in spreads.items():
        noise = np.random.default_rng([zlib.crc32(name.encode()), seed]).standard_normal(out[name].shape)
        drawn = base * np.exp(spread * noise) if base else spread * noise
        out[name] = jnp.asarray(drawn.astype(out[name].dtype))
    for name, factor in factors.items():
        out[name] = (out[name] * factor).astype(out[name].dtype)
    return out
```

```python
from contextlib import ExitStack

import concourse.bass as bass
from concourse import mybir

F32 = mybir.dt.float32
F16 = mybir.dt.float16
ALU = mybir.AluOpType
ACT = mybir.ActivationFunctionType
AXX = mybir.AxisListType.X

P = 128
N = 4096
D = 256
TILES = N // P
GROUP = 512
GROUPS = N // GROUP
GT = GROUP // P
CT = 4
CHUNKS = TILES // CT
CW = CT * GROUP
GD = GT * D
KD = D // P
RAW = 4
CUT = 2
A_UP = 4096.0
F_UP = 64.0
DOWN = 1.0 / (A_UP * F_UP)
LN_EPS = 1e-5
DEG_EPS = 1e-8
CONV1, CONV2, HEADS, NORM, LAST = range(5)
LAYERS = 5


def gnn_kernel(nc, x, xT, adjT, w1, w2, wh, w2a, w2b, w3, b1, b2, bh, b2a, b2b, b3, out):
    x_t = x.rearrange("(g j p) d -> g p j d", p=P, j=GT)
    xT_t = xT.rearrange("(k p) (g n) -> g p k n", p=P, n=GROUP)
    out_t = out.rearrange("(g j p) d -> g p j d", p=P, j=GT)

    with ExitStack() as ctx:
        def sb(name, shape, dt):
            return ctx.enter_context(nc.sbuf_tensor(name, shape, dt))

        def ps(name, shape):
            return ctx.enter_context(nc.psum_tensor(name, shape, F32))

        def sem(name):
            return ctx.enter_context(nc.semaphore(name))

        raw = sb("raw", [P, RAW, CW], F32)
        a_hi = sb("a_hi", [P, CUT, CW], F16)
        a_lo = sb("a_lo", [P, CUT, CW], F16)
        xs = sb("xs", [P, TILES, D], F32)
        f_hi = sb("f_hi", [P, 2, TILES, D], F16)
        f_lo = sb("f_lo", [P, 2, TILES, D], F16)
        agg = sb("agg", [P, KD, GROUP], F32)
        side = sb("side", [P, KD, GROUP], F32)
        u = sb("u", [P, GT, D], F32)
        v = sb("v", [P, GT, D], F32)
        w = sb("w", [P, GT, D], F32)
        x_in = sb("x_in", [P, GT, D], F32)
        colw = sb("colw", [P, CW], F32)
        col = sb("col", [P, GROUP], F32)
        w1_s = sb("w1_s", [P, 2 * KD, D], F32)
        w2_s = sb("w2_s", [P, 2 * KD, D], F32)
        wh_s = sb("wh_s", [P, KD, D], F32)
        w2a_s = sb("w2a_s", [P, KD, P], F32)
        w2b_s = sb("w2b_s", [P, D], F32)
        w3_s = sb("w3_s", [P, KD, D], F32)
        b1_s = sb("b1_s", [P, D], F32)
        b2_s = sb("b2_s", [P, D], F32)
        bh_s = sb("bh_s", [P, D], F32)
        b2a_s = sb("b2a_s", [P, P], F32)
        b2b_s = sb("b2b_s", [P, D], F32)
        b3_s = sb("b3_s", [P, D], F32)
        ident = sb("ident", [P, P], F32)
        ident_up = sb("ident_up", [P, P], F16)
        ones = sb("ones", [P, 1], F32)
        ln_eps = sb("ln_eps", [P, 1], F32)
        deg_eps = sb("deg_eps", [P, 1], F32)
        zero = sb("zero", [P, 1], F32)
        deg = sb("deg", [P, TILES], F32)
        none = sb("none", [P, GT], F32)
        root = sb("root", [P, 2, GT], F32)
        r_norm = sb("r_norm", [P, TILES], F32)
        r_last = sb("r_last", [P, TILES], F32)
        adj_r = sb("adj_r", [P, TILES], F32)
        stats = sb("stats", [P, GT, 6], F32)
        mv = sb("mv", [P, GT, 2], F32)
        std = sb("std", [P, GT], F32)
        rstd = sb("rstd", [P, GT], F32)

        main = [ps("main0", [P, GROUP]), ps("main1", [P, GROUP])]
        p_turn = ps("p_turn", [P, KD, GROUP])
        p_y = ps("p_y", [P, GT, D])
        p_h = ps("p_h", [P, GT, P])
        p_col = ps("p_col", [P, GROUP])

        consts_set = sem("consts_set")
        ident_zero = sem("ident_zero")
        weights_in = sem("weights_in")
        x_piece_in = [sem(f"x_piece_in{c}") for c in range(CHUNKS)]
        raw_in = [sem(f"raw_in{s}") for s in range(RAW)]
        side_in = sem("side_in")
        x_again_in = sem("x_again_in")
        hi_cut = sem("hi_cut")
        lo_cut = sem("lo_cut")
        raw_read = sem("raw_read")
        chunk_used = sem("chunk_used")
        half0_done = sem("half0_done")
        half_out = [sem("half0_out"), sem("half1_out")]
        fhi_set = sem("fhi_set")
        flo_set = sem("flo_set")
        y_done = sem("y_done")
        y_read = sem("y_read")
        v_set = sem("v_set")
        v_part = sem("v_part")
        relu_set = sem("relu_set")
        u_set = sem("u_set")
        turned = sem("turned")
        turn_out = [sem("turn0_out"), sem("turn1_out")]
        h_done = sem("h_done")
        stats_set = sem("stats_set")
        mv_set = sem("mv_set")
        std_set = sem("std_set")
        rstd_set = sem("rstd_set")
        x_new = sem("x_new")
        x_kept = sem("x_kept")
        w_part = sem("w_part")
        w_set = sem("w_set")
        col_step = sem("col_step")
        col_set = sem("col_set")
        col_done = sem("col_done")
        deg_set = sem("deg_set")
        none_set = sem("none_set")
        root_in = sem("root_in")
        root_set = sem("root_set")
        recip_set = sem("recip_set")
        r_set = sem("r_set")
        adj_r_set = sem("adj_r_set")
        extra_set = sem("extra_set")
        out_set = sem("out_set")
        out_written = sem("out_written")

        def tail_of(l, g):
            if is_first(g):
                return l - 1, GROUPS - 1
            return l, g - 1

        def is_first(g):
            return isinstance(g, int) and g == 0

        def free(eng, semaphore, count):
            if not is_first(count):
                eng.wait_ge(semaphore, count)

        def rows(t, g):
            return t[:, bass.ds(g * GT, GT)]

        def run(eng, group, last):
            for l in range(LAYERS):
                group(l, 0)
                group(l, 1)
                with eng.Fori(2, GROUPS) as g:
                    group(l, g)
            last(LAYERS - 1, GROUPS - 1)

        block = ctx.enter_context(nc.Block())


        @block.gpsimd
        def _(pool):
            nc.gpsimd.memset(ident[:], 0.0)
            nc.gpsimd.memset(ident_up[:], 0.0).then_inc(ident_zero, 1)
            nc.gpsimd.memset(ones[:], 1.0)
            nc.gpsimd.memset(ln_eps[:], LN_EPS)
            nc.gpsimd.memset(zero[:], 0.0)
            nc.gpsimd.memset(deg_eps[:], DEG_EPS).then_inc(consts_set, 1)
            pool.wait_ge(ident_zero, 1)
            nc.gpsimd.affine_select(out=ident[:], in_=ident[:], compare_op=ALU.not_equal, fill=1.0,
                                    base=0, pattern=[[-1, P]], channel_multiplier=1).then_inc(consts_set, 1)
            nc.gpsimd.affine_select(out=ident_up[:], in_=ident_up[:], compare_op=ALU.not_equal, fill=A_UP,
                                    base=0, pattern=[[-1, P]], channel_multiplier=1).then_inc(consts_set, 1)

        @block.sync
        def _(sp):
            def stream(l, g, c):
                k = (l * GROUPS + g) * CHUNKS + c
                if not (l == 0 and is_first(g) and c < RAW):
                    sp.wait_ge(hi_cut, k - RAW + 1)
                    sp.wait_ge(lo_cut, k - RAW + 1)
                sp.dma_start(raw[:, c % RAW, :], adjT[g, c]).then_inc(raw_in[c % RAW], 16)

            def load_side(g):
                free(sp, y_done, g)
                sp.dma_start(side[:], xT_t[g]).then_inc(side_in, 16)

            def load_x_again(g):
                if not is_first(g):
                    sp.wait_ge(v_set, GROUPS + g)
                sp.dma_start(x_in[:], x_t[g]).then_inc(x_again_in, 16)

            def store(g):
                sp.wait_ge(out_set, g + 1)
                sp.dma_start(out_t[g], u[:]).then_inc(out_written, 16)

            def group(l, g):
                tl, tg = tail_of(l, g)
                for c in range(CHUNKS):
                    if l == 0 and is_first(g):
                        sp.dma_start(xs[:, c * GT:(c + 1) * GT, :], x_t[c]).then_inc(x_piece_in[c], 16)
                    stream(l, g, c)
                    if l == 0 and is_first(g) and c == 1:
                        for dst, src in ((w1_s, w1), (w2_s, w2), (wh_s, wh), (w2a_s, w2a), (w3_s, w3)):
                            sp.dma_start(dst[:], src.rearrange("(k p) n -> p k n", p=P)).then_inc(weights_in, 16)
                        sp.dma_start(w2b_s[:], w2b).then_inc(weights_in, 16)
                        for dst, src in ((b1_s, b1), (b2_s, b2), (bh_s, bh), (b2a_s, b2a), (b2b_s, b2b), (b3_s, b3)):
                            sp.dma_start(dst[:], src.partition_broadcast(P)).then_inc(weights_in, 16)
                    if tl >= 0 and c == 0:
                        if tl == CONV1:
                            load_side(tg)
                        if tl == CONV2:
                            load_x_again(tg)
                    if tl == LAST and c == 5:
                        store(tg)

            run(sp, group, lambda tl, tg: store(tg))
            sp.wait_ge(out_written, 16 * GROUPS)

        WEIGHTS = 16 * 12

        @block.tensor
        def _(pe):
            def stream(l, g, c):
                k = (l * GROUPS + g) * CHUNKS + c
                slot, buf = c % CUT, l % 2
                pe.wait_ge(fhi_set, l * GROUPS + c + 1)
                pe.wait_ge(flo_set, l * GROUPS + c + 1)
                pe.wait_ge(hi_cut, k + 1)
                pe.wait_ge(lo_cut, k + 1)
                for h in range(2):
                    if c == 0 and not (l == 0 and is_first(g)):
                        pe.wait_ge(half_out[h], l * GROUPS + g)
                    for t in range(CT):
                        m = c * CT + t
                        if l == NORM:
                            at = slice(t * GROUP + h * D, t * GROUP + (h + 1) * D)
                            feat, o = slice(0, P), main[h][:, 0:D]
                        else:
                            at = slice(t * GROUP, (t + 1) * GROUP)
                            feat, o = slice(h * P, (h + 1) * P), main[h][:]
                        end = c == CHUNKS - 1 and t == CT - 1 and l != NORM
                        nc.tensor.matmul(o, f_hi[:, buf, m, feat], a_hi[:, slot, at], start=(m == 0), stop=False)
                        nc.tensor.matmul(o, f_hi[:, buf, m, feat], a_lo[:, slot, at], start=False, stop=False)
                        last = nc.tensor.matmul(o, f_lo[:, buf, m, feat], a_hi[:, slot, at], start=False, stop=end)
                    if c == CHUNKS - 1:
                        if l == NORM:
                            if h == 0:
                                pe.wait_ge(consts_set, 3)
                            for j in (2 * h, 2 * h + 1):
                                for n, part in enumerate((f_hi, f_lo)):
                                    o = main[h][:, (j % 2) * P:(j % 2 + 1) * P]
                                    last = nc.tensor.matmul(o, part[:, buf, bass.ds(g * GT + j, 1), 0:P].rearrange("p a b -> p (a b)"),
                                                            ident_up[:], start=False,
                                                            stop=(j % 2 == 1 and n == 1))
                        if h == 0:
                            last.then_inc(half0_done, 1)
                last.then_inc(chunk_used, 1)

            def turn(tl, tg):
                count = (GROUPS if tl == HEADS else 0) + tg + 1
                if tl == CONV2:
                    pe.wait_ge(u_set, tg + 1)
                else:
                    pe.wait_ge(x_new, count)
                pe.wait_ge(consts_set, 3)
                for h in range(2):
                    free(pe, turn_out[h], count - 1)
                for h in range(KD):
                    for j in range(GT):
                        last = nc.tensor.transpose(p_turn[:, h, j * P:(j + 1) * P], u[:, j, h * P:(h + 1) * P], ident[:])
                last.then_inc(turned, 1)

            def product(tl, tg):
                n = tl * GROUPS + tg
                pe.wait_ge(half_out[0], n + 1)
                pe.wait_ge(half_out[1], n + 1)
                free(pe, v_set, n)
                if tl == CONV1:
                    pe.wait_ge(side_in, 16 * (tg + 1))
                    pe.wait_ge(weights_in, WEIGHTS)
                if tl == CONV2:
                    pe.wait_ge(turn_out[0], tg + 1)
                    pe.wait_ge(turn_out[1], tg + 1)
                parts = {CONV1: [(side, 0, w1_s[:, 0]), (side, 1, w1_s[:, 1]), (agg, 0, w1_s[:, 2]), (agg, 1, w1_s[:, 3])],
                         CONV2: [(side, 0, w2_s[:, 0]), (side, 1, w2_s[:, 1]), (agg, 0, w2_s[:, 2]), (agg, 1, w2_s[:, 3])],
                         HEADS: [(agg, 0, wh_s[:, 0]), (agg, 1, wh_s[:, 1])],
                         NORM: [(agg, 0, w2b_s[:])],
                         LAST: [(agg, 0, w3_s[:, 0]), (agg, 1, w3_s[:, 1])]}[tl]
                for j in range(GT):
                    for i, (t, k, wt) in enumerate(parts):
                        last = nc.tensor.matmul(p_y[:, j, :], t[:, k, j * P:(j + 1) * P], wt,
                                                start=(i == 0), stop=(i == len(parts) - 1))
                last.then_inc(y_done, 1)

            def hidden(tg):
                pe.wait_ge(turn_out[0], GROUPS + tg + 1)
                pe.wait_ge(turn_out[1], GROUPS + tg + 1)
                free(pe, w_part, tg)
                for j in range(GT):
                    for k in range(KD):
                        last = nc.tensor.matmul(p_h[:, j, :], side[:, k, j * P:(j + 1) * P], w2a_s[:, k],
                                                start=(k == 0), stop=(k == KD - 1))
                last.then_inc(h_done, 1)

            def columns(tl, tg):
                n = (tl - CONV2) * GROUPS + tg
                pe.wait_ge(col_set, n + 1)
                if is_first(n):
                    pe.wait_ge(consts_set, 1)
                free(pe, deg_set, tg if tl == CONV2 else GROUPS)
                if tl == HEADS:
                    free(pe, adj_r_set, tg)
                for j in range(GT):
                    last = nc.tensor.matmul(p_col[:, j:j + 1], col[:, j * P:(j + 1) * P], ones[:], start=True, stop=True)
                last.then_inc(col_done, 1)

            def tail(tl, tg, c):
                if tl < 0:
                    return
                if tl in (CONV2, HEADS) and c == 0:
                    columns(tl, tg)
                if tl == CONV2 and c == 0:
                    turn(tl, tg)
                if c == (2 if tl == CONV2 else 1):
                    product(tl, tg)
                if tl == HEADS and c == 4:
                    turn(tl, tg)
                if tl == HEADS and c == 5:
                    hidden(tg)

            def group(l, g):
                tl, tg = tail_of(l, g)
                for c in range(CHUNKS):
                    stream(l, g, c)
                    tail(tl, tg, c)

            def last(tl, tg):
                for c in range(CHUNKS):
                    tail(tl, tg, c)

            run(pe, group, last)

        @block.scalar
        def _(act):
            def first_features(c):
                act.wait_ge(x_piece_in[c], 16)
                nc.scalar.activation(f_hi[:, 0, c * GT:(c + 1) * GT, :], xs[:, c * GT:(c + 1) * GT, :], ACT.Copy,
                                     scale=F_UP).then_inc(fhi_set, 1)

            def stream(l, g, c):
                k = (l * GROUPS + g) * CHUNKS + c
                act.wait_ge(raw_in[c % RAW], 16 * ((l * GROUPS + g) * (CHUNKS // RAW) + c // RAW + 1))
                if not (l == 0 and is_first(g) and c < CUT):
                    act.wait_ge(chunk_used, k - CUT + 1)
                nc.scalar.activation(a_hi[:, c % CUT, :], raw[:, c % RAW, :], ACT.Copy, scale=A_UP).then_inc(hi_cut, 1)

            def tail(tl, tg, c):
                if tl < 0:
                    return
                n = tl * GROUPS + tg
                if c == 0:
                    if tl == CONV2:
                        free(act, turned, tg)
                        nc.scalar.activation(u[:], rows(xs, tg), ACT.Copy).then_inc(u_set, 1)
                    act.wait_ge(half0_done, n + 1)
                    if tl == NORM:
                        act_out = agg[:, 0, 0:D]
                        act_in = main[0][:, 0:D]
                    else:
                        act_out, act_in = agg[:, 0, :], main[0][:]
                    free(act, y_done, n)
                    nc.scalar.activation(act_out, act_in, ACT.Copy, scale=DOWN).then_inc(half_out[0], 1)
                if (tl == CONV2 and c == 1) or (tl == HEADS and c == 4):
                    count = (GROUPS if tl == HEADS else 0) + tg + 1
                    act.wait_ge(turned, count)
                    if tl == HEADS:
                        free(act, h_done, tg)
                    nc.scalar.activation(side[:, 0, :], p_turn[:, 0, :], ACT.Copy).then_inc(turn_out[0], 1)
                if tl == CONV1 and c == 2:
                    act.wait_ge(v_set, n + 1)
                    nc.scalar.activation(rows(xs, tg), v[:], ACT.Relu).then_inc(relu_set, 1)
                    nc.scalar.activation(f_hi[:, 1, bass.ds(tg * GT, GT), :], v[:], ACT.Relu, scale=F_UP).then_inc(fhi_set, 1)
                if tl in (CONV2, HEADS, NORM, LAST) and c == (3 if tl == CONV2 else 2):
                    act.wait_ge(mv_set, (tl - CONV2) * GROUPS + tg + 1)
                    nc.scalar.activation(std[:], mv[:, :, 1:2].rearrange("p a b -> p (a b)"), ACT.Sqrt,
                                         bias=ln_eps[:]).then_inc(std_set, 1)
                if tl == CONV2 and c == 4:
                    act.wait_ge(x_new, tg + 1)
                    nc.scalar.activation(f_hi[:, 0, bass.ds(tg * GT, GT), :], rows(xs, tg), ACT.Copy,
                                         scale=F_UP).then_inc(fhi_set, 1)
                if tl in (HEADS, NORM) and c == 3:
                    act.wait_ge(x_new, (tl - CONV2) * GROUPS + tg + 1)
                    nc.scalar.activation(rows(xs, tg), u[:], ACT.Copy).then_inc(x_kept, 1)
                if tl in (HEADS, NORM) and c == (5 if tl == HEADS else 4):
                    act.wait_ge(w_set, (tl - HEADS) * GROUPS + tg + 1)
                    wide = P if tl == HEADS else D
                    nc.scalar.activation(f_hi[:, (tl + 1) % 2, bass.ds(tg * GT, GT), 0:wide], w[:, :, 0:wide], ACT.Copy,
                                         scale=F_UP).then_inc(fhi_set, 1)
                if tl == CONV2 and c == 2:
                    act.wait_ge(root_in, tg + 1)
                    nc.scalar.activation(root[:, 0, :], root[:, 0, :], ACT.Sqrt, bias=zero[:]).then_inc(root_set, 1)
                    nc.scalar.activation(root[:, 1, :], rows(deg, tg), ACT.Sqrt, bias=deg_eps[:]).then_inc(root_set, 1)

            def group(l, g):
                tl, tg = tail_of(l, g)
                if l == 0 and is_first(g):
                    act.wait_ge(consts_set, 1)
                for c in range(CHUNKS):
                    if l == 0 and is_first(g):
                        first_features(c)
                    stream(l, g, c)
                    tail(tl, tg, c)

            def last(tl, tg):
                for c in range(CHUNKS):
                    tail(tl, tg, c)

            run(act, group, last)

        @block.vector
        def _(dve):
            def cut_low(dst, src, upper, up):
                return nc.vector.scalar_tensor_tensor(out=dst, in0=src, scalar=up, in1=upper,
                                                      op0=ALU.mult, op1=ALU.subtract)

            def first_features(c):
                at = slice(c * GT, (c + 1) * GT)
                dve.wait_ge(x_piece_in[c], 16)
                dve.wait_ge(fhi_set, c + 1)
                cut_low(f_lo[:, 0, at, :].rearrange("p a b -> p (a b)"), xs[:, at, :].rearrange("p a b -> p (a b)"),
                        f_hi[:, 0, at, :].rearrange("p a b -> p (a b)"), F_UP).then_inc(flo_set, 1)

            def stream(l, g, c):
                k = (l * GROUPS + g) * CHUNKS + c
                chunk = raw[:, c % RAW, :]
                dve.wait_ge(raw_in[c % RAW], 16 * ((l * GROUPS + g) * (CHUNKS // RAW) + c // RAW + 1))
                if l == CONV2:
                    n = g * (CHUNKS + 1)
                    if c == 0:
                        free(dve, col_set, g)
                        nc.vector.tensor_copy(colw[:], chunk).then_inc(col_step, 1)
                    else:
                        dve.wait_ge(col_step, n + c)
                        nc.vector.tensor_tensor(colw[:], colw[:], chunk, ALU.add).then_inc(col_step, 1)
                    if c == CHUNKS - 1:
                        dve.wait_ge(col_step, n + CHUNKS)
                        nc.vector.tensor_tensor(colw[:, 0:2 * GROUP], colw[:, 0:2 * GROUP], colw[:, 2 * GROUP:],
                                                ALU.add).then_inc(col_step, 1)
                        dve.wait_ge(col_step, n + CHUNKS + 1)
                        free(dve, col_done, g)
                        nc.vector.tensor_tensor(col[:], colw[:, 0:GROUP], colw[:, GROUP:2 * GROUP],
                                                ALU.add).then_inc(col_set, 1)
                if l == HEADS:
                    n0 = GROUPS * (CHUNKS + 1) + g * (TILES - 1)
                    dve.wait_ge(r_set, c + 1 if is_first(g) else GROUPS)
                    for t in range(CT):
                        m = c * CT + t
                        scaled = raw[:, c % RAW, t * GROUP:(t + 1) * GROUP]
                        r = r_norm[:, m:m + 1]
                        if m == 0:
                            dve.wait_ge(col_set, GROUPS + g)
                            nc.vector.tensor_scalar(colw[:, 0:GROUP], scaled, r, None, ALU.mult).then_inc(col_step, 1)
                            continue
                        dve.wait_ge(col_step, n0 + m)
                        into, done = (col, col_set) if m == TILES - 1 else (colw, col_step)
                        if m == TILES - 1:
                            dve.wait_ge(col_done, GROUPS + g)
                        nc.vector.scalar_tensor_tensor(out=into[:, 0:GROUP], in0=scaled, scalar=r, in1=colw[:, 0:GROUP],
                                                       op0=ALU.mult, op1=ALU.add).then_inc(done, 1)
                dve.wait_ge(hi_cut, k + 1)
                if not (l == 0 and is_first(g) and c < CUT):
                    dve.wait_ge(chunk_used, k - CUT + 1)
                cut_low(a_lo[:, c % CUT, :], chunk, a_hi[:, c % CUT, :], A_UP).then_inc(lo_cut, 1)

            def flat(t):
                return t.rearrange("p a b -> p (a b)")

            def bias(t):
                return t[:].unsqueeze(1).to_broadcast([P, GT, t.shape[1]])

            def norm(tl, tg, dst, gate=None):
                n = (tl - CONV2) * GROUPS + tg
                dve.wait_ge(v_set, tl * GROUPS + tg + 1)
                for j in range(GT):
                    last = nc.vector.bn_stats(stats[:, j, :], v[:, j, :])
                last.then_inc(stats_set, 1)
                dve.wait_ge(consts_set, 1)
                dve.wait_ge(stats_set, n + 1)
                for j in range(GT):
                    last = nc.vector.bn_aggr(mv[:, j, :], stats[:, j, :])
                last.then_inc(mv_set, 1)
                dve.wait_ge(std_set, n + 1)
                nc.vector.reciprocal(rstd[:], std[:]).then_inc(rstd_set, 1)
                dve.wait_ge(rstd_set, n + 1)
                for j in range(GT):
                    last = nc.vector.tensor_scalar(dst(j), v[:, j, :], mv[:, j, 0:1], rstd[:, j:j + 1],
                                                   ALU.subtract, ALU.mult)
                return last

            def cut_w(tl, tg, count):
                wide = P if tl == HEADS else D
                dve.wait_ge(fhi_set, (tl + 1) * GROUPS + tg + 1)
                nc.vector.scalar_tensor_tensor(out=f_lo[:, (tl + 1) % 2, bass.ds(tg * GT, GT), 0:wide],
                                               in0=w[:, :, 0:wide], scalar=F_UP,
                                               in1=f_hi[:, (tl + 1) % 2, bass.ds(tg * GT, GT), 0:wide],
                                               op0=ALU.mult, op1=ALU.subtract).then_inc(flo_set, 1)

            def tail(tl, tg, c):
                if tl < 0:
                    return
                n = tl * GROUPS + tg
                if c == 0:
                    dve.wait_ge(chunk_used, CHUNKS * (n + 1))
                    free(dve, y_done, n)
                    if tl == NORM:
                        o, i = agg[:, 0, D:2 * D], main[1][:, 0:D]
                    else:
                        o, i = agg[:, 1, :], main[1][:]
                    nc.vector.tensor_scalar(o, i, DOWN, None, ALU.mult).then_inc(half_out[1], 1)
                if (tl == CONV2 and c == 1) or (tl == HEADS and c == 4):
                    count = (GROUPS if tl == HEADS else 0) + tg + 1
                    dve.wait_ge(turned, count)
                    if tl == HEADS:
                        free(dve, h_done, tg)
                    nc.vector.tensor_copy(side[:, 1, :], p_turn[:, 1, :]).then_inc(turn_out[1], 1)
                if tl == CONV2 and c == 1:
                    dve.wait_ge(col_done, tg + 1)
                    nc.vector.tensor_copy(rows(deg, tg), p_col[:, 0:GT]).then_inc(deg_set, 1)
                    dve.wait_ge(deg_set, tg + 1)
                    free(dve, r_set, tg)
                    nc.vector.tensor_scalar(none[:], rows(deg, tg), 1.0, 0.0, ALU.add, ALU.is_equal).then_inc(none_set, 1)
                    dve.wait_ge(none_set, 2 * tg + 1)
                    nc.vector.scalar_tensor_tensor(out=root[:, 0, :], in0=rows(deg, tg), scalar=1.0, in1=none[:],
                                                   op0=ALU.add, op1=ALU.add).then_inc(root_in, 1)
                if tl == CONV2 and c == 2:
                    dve.wait_ge(root_set, 2 * tg + 2)
                    nc.vector.reciprocal(root[:], root[:]).then_inc(recip_set, 1)
                    nc.vector.tensor_scalar(none[:], none[:], -1.0, 1.0, ALU.mult, ALU.add).then_inc(none_set, 1)
                    dve.wait_ge(recip_set, tg + 1)
                    dve.wait_ge(none_set, 2 * tg + 2)
                    nc.vector.tensor_copy(rows(r_last, tg), root[:, 1, :])
                    nc.vector.tensor_tensor(rows(r_norm, tg), root[:, 0, :], none[:], ALU.mult).then_inc(r_set, 1)
                if tl == HEADS and c == 1:
                    dve.wait_ge(col_done, GROUPS + tg + 1)
                    nc.vector.tensor_copy(rows(adj_r, tg), p_col[:, 0:GT]).then_inc(adj_r_set, 1)
                if tl == CONV1 and c == 2:
                    dve.wait_ge(y_done, n + 1)
                    free(dve, fhi_set, GROUPS + tg)
                    free(dve, relu_set, tg)
                    nc.vector.tensor_tensor(v[:], p_y[:], bias(b1_s), ALU.add).then_inc(v_set, 1)
                if tl == CONV1 and c == 3:
                    dve.wait_ge(relu_set, tg + 1)
                    dve.wait_ge(fhi_set, GROUPS + tg + 1)
                    at = bass.ds(tg * GT, GT)
                    cut_low(f_lo[:, 1, at, :], xs[:, at, :], f_hi[:, 1, at, :], F_UP).then_inc(flo_set, 1)
                if tl == CONV2 and c == 3:
                    dve.wait_ge(y_done, n + 1)
                    nc.vector.tensor_tensor(v[:], p_y[:], bias(b2_s), ALU.add).then_inc(y_read, 1)
                    dve.wait_ge(y_read, n - GROUPS + 1)
                    nc.vector.scalar_tensor_tensor(out=v[:], in0=v[:], scalar=0.0, in1=rows(xs, tg), op0=ALU.max,
                                                   op1=ALU.add).then_inc(v_part, 1)
                    dve.wait_ge(v_part, tg + 1)
                    dve.wait_ge(x_again_in, 16 * (tg + 1))
                    nc.vector.scalar_tensor_tensor(out=v[:], in0=v[:], scalar=0.0, in1=x_in[:], op0=ALU.max,
                                                   op1=ALU.add).then_inc(v_set, 1)
                    norm(tl, tg, lambda j: xs[:, bass.ds(tg * GT + j, 1), :].rearrange("p a b -> p (a b)")).then_inc(x_new, 1)
                if tl == CONV2 and c == 4:
                    dve.wait_ge(fhi_set, 2 * GROUPS + tg + 1)
                    at = bass.ds(tg * GT, GT)
                    cut_low(f_lo[:, 0, at, :], xs[:, at, :], f_hi[:, 0, at, :], F_UP).then_inc(flo_set, 1)
                if tl == HEADS and c == 2:
                    dve.wait_ge(y_done, n + 1)
                    nc.vector.tensor_tensor(v[:], p_y[:], bias(bh_s), ALU.add).then_inc(y_read, 1)
                    dve.wait_ge(y_read, n - GROUPS + 1)
                    nc.vector.tensor_tensor(v[:], v[:], rows(xs, tg), ALU.add).then_inc(v_set, 1)
                    dve.wait_ge(turned, GROUPS + tg)
                    free(dve, x_kept, tg)
                    norm(tl, tg, lambda j: u[:, j, :]).then_inc(x_new, 1)
                if tl == HEADS and c == 5:
                    dve.wait_ge(h_done, tg + 1)
                    dve.wait_ge(fhi_set, 3 * GROUPS + tg)
                    dve.wait_ge(flo_set, 3 * GROUPS + tg)
                    nc.vector.tensor_tensor(w[:, :, 0:P], p_h[:], bias(b2a_s), ALU.add).then_inc(w_part, 1)
                    dve.wait_ge(w_part, tg + 1)
                    nc.vector.tensor_tensor(w[:, :, 0:P], w[:, :, 0:P],
                                            rows(r_norm, tg).unsqueeze(2).to_broadcast([P, GT, P]),
                                            ALU.mult).then_inc(w_set, 1)
                    cut_w(tl, tg, 0)
                if tl == NORM and c == 2:
                    dve.wait_ge(y_done, n + 1)
                    nc.vector.tensor_tensor(none[:], rows(adj_r, tg), rows(r_norm, tg), ALU.add).then_inc(extra_set, 1)
                    dve.wait_ge(extra_set, 2 * tg + 1)
                    for j in range(GT):
                        last = nc.vector.scalar_tensor_tensor(out=v[:, j, :], in0=b2b_s[:], scalar=none[:, j:j + 1],
                                                              in1=p_y[:, j, :], op0=ALU.mult, op1=ALU.add)
                    last.then_inc(y_read, 1)
                    dve.wait_ge(y_read, n - GROUPS + 1)
                    nc.vector.tensor_tensor(v[:], v[:], rows(r_norm, tg).unsqueeze(2).to_broadcast([P, GT, D]),
                                            ALU.mult).then_inc(extra_set, 1)
                    dve.wait_ge(extra_set, 2 * tg + 2)
                    nc.vector.tensor_tensor(v[:], v[:], rows(xs, tg), ALU.add).then_inc(v_set, 1)
                    dve.wait_ge(x_kept, GROUPS + tg)
                    norm(tl, tg, lambda j: u[:, j, :]).then_inc(x_new, 1)
                    dve.wait_ge(x_new, 2 * GROUPS + tg + 1)
                    dve.wait_ge(fhi_set, 4 * GROUPS + tg)
                    dve.wait_ge(flo_set, 4 * GROUPS + tg)
                    nc.vector.tensor_tensor(w[:], u[:], rows(r_last, tg).unsqueeze(2).to_broadcast([P, GT, D]),
                                            ALU.mult).then_inc(w_set, 1)
                if tl == NORM and c == 3:
                    dve.wait_ge(w_set, GROUPS + tg + 1)
                    cut_w(tl, tg, 0)
                if tl == LAST and c == 2:
                    dve.wait_ge(y_done, n + 1)
                    free(dve, out_set, tg)
                    nc.vector.tensor_tensor(v[:], p_y[:], rows(r_last, tg).unsqueeze(2).to_broadcast([P, GT, D]),
                                            ALU.mult).then_inc(y_read, 1)
                    dve.wait_ge(y_read, n - GROUPS + 1)
                    nc.vector.tensor_tensor(v[:], v[:], bias(b3_s), ALU.add).then_inc(v_part, 1)
                    dve.wait_ge(v_part, GROUPS + tg + 1)
                    nc.vector.tensor_tensor(v[:], v[:], rows(xs, tg), ALU.add).then_inc(v_set, 1)
                    dve.wait_ge(x_kept, 2 * GROUPS)
                    free(dve, out_written, 16 * tg)
                    norm(tl, tg, lambda j: u[:, j, :]).then_inc(out_set, 1)

            def group(l, g):
                tl, tg = tail_of(l, g)
                for c in range(CHUNKS):
                    if l == 0 and is_first(g):
                        first_features(c)
                    stream(l, g, c)
                    tail(tl, tg, c)

            def last(tl, tg):
                for c in range(CHUNKS):
                    tail(tl, tg, c)

            run(dve, group, last)


_INS = ["x", "xT", "adjT", "w1", "w2", "wh", "w2a", "w2b", "w3", "b1", "b2", "bh", "b2a", "b2b", "b3"]


def kernel(x, adj, L0_gnn_W1, L0_gnn_b1, L0_gnn_W2, L0_gnn_b2, L1_gnn_W, L1_gnn_b, L2_gnn_W1, L2_gnn_b1,
           L2_gnn_W2, L2_gnn_b2, L3_gnn_W, L3_gnn_b):
    import numpy as np
    import concourse.bacc as bacc
    from concourse.bass_utils import run_bass_kernel_spmd

    x, adj = np.asarray(x), np.asarray(adj)
    heads = np.asarray(L1_gnn_W)
    data = {
        "x": x,
        "xT": x.T,
        "adjT": adj.reshape(GROUPS, GROUP, CHUNKS, CT, P).transpose(0, 2, 4, 3, 1).reshape(GROUPS, CHUNKS, P, CW),
        "w1": np.asarray(L0_gnn_W1),
        "w2": np.asarray(L0_gnn_W2),
        "wh": heads.transpose(1, 0, 2).reshape(D, D),
        "w2a": np.asarray(L2_gnn_W1).T,
        "w2b": np.asarray(L2_gnn_W2).T,
        "w3": np.asarray(L3_gnn_W).T,
        "b1": np.asarray(L0_gnn_b1),
        "b2": np.asarray(L0_gnn_b2),
        "bh": np.asarray(L1_gnn_b).reshape(D),
        "b2a": np.asarray(L2_gnn_b1),
        "b2b": np.asarray(L2_gnn_b2),
        "b3": np.asarray(L3_gnn_b),
    }
    nc = bacc.Bacc("TRN2", target_bir_lowering=False, num_devices=1)
    arrays, args = {}, []
    for name in _INS:
        a = np.ascontiguousarray(data[name])
        arrays[f"in_{name}"] = a
        args.append(nc.dram_tensor(f"in_{name}", a.shape, mybir.dt.from_np(a.dtype), kind="ExternalInput").ap())
    args.append(nc.dram_tensor("out", (N, D), F32, kind="ExternalOutput").ap())
    gnn_kernel(nc, *args)
    r = run_bass_kernel_spmd(nc, [arrays], core_ids=[0])
    return r.results[0]["out"]
```

```python
from contextlib import ExitStack

import concourse.bass as bass
from concourse import mybir

F32 = mybir.dt.float32
F16 = mybir.dt.float16
F8 = mybir.dt.float8e4
U32 = mybir.dt.uint32
U8 = mybir.dt.uint8
BF16 = mybir.dt.bfloat16
I32 = mybir.dt.int32
ALU = mybir.AluOpType
ACT = mybir.ActivationFunctionType
AXX = mybir.AxisListType.X

P = 128
N = 4096
D = 256
TILES = N // P
GROUP = 512
GROUPS = N // GROUP
GT = GROUP // P
CT = 4
CHUNKS = TILES // CT
CW = CT * GROUP
GD = GT * D
KD = D // P
RAW = 4
CUT = 2
A_UP = 4096.0
F_UP = 64.0
DOWN = 1.0 / (A_UP * F_UP)
LN_EPS = 1e-5
DEG_EPS = 1e-8
PAIR = 2
LOADS = CHUNKS // PAIR
CONV1, CONV2, HEADS, NORM, LAST = range(5)
LAYERS = 5


def gnn_kernel(nc, x, xT, adjT, diag, diagT, w1, w2, wh, w2a, w2b, w3, b1, b2, bh, b2a, b2b, b3, out):
    x_t = x.rearrange("(g j p) d -> g p j d", p=P, j=GT)
    xT_t = xT.rearrange("(k p) (g n) -> g p k n", p=P, n=GROUP)
    out_t = out.rearrange("(g j p) d -> g p j d", p=P, j=GT)

    with ExitStack() as ctx:
        def sb(name, shape, dt):
            return ctx.enter_context(nc.sbuf_tensor(name, shape, dt))

        def ps(name, shape):
            return ctx.enter_context(nc.psum_tensor(name, shape, F32))

        def sem(name):
            return ctx.enter_context(nc.semaphore(name))

        raw = sb("raw", [P, RAW, CW], F32)
        mask_in_ring = raw[:, 0:2, :].rearrange("p s c -> p (s c)").bitcast(F8).rearrange(
            "p (q i c) -> p q i c", q=LOADS, i=PAIR)
        mask_made_ring = sb("mask_made_ring", [P, RAW, CW], F8)
        cut = sb("cut", [P, 2, CUT, CW], F16)
        a_hi, a_lo = cut[:, 0], cut[:, 1]
        value_cols = cut[:, :].rearrange("p a b c -> p (a b c)").bitcast(F32)
        xs = sb("xs", [P, TILES, D], F32)
        f_hi = sb("f_hi", [P, 2, TILES, D], F16)
        f_lo = sb("f_lo", [P, 2, TILES, D], F16)
        agg = sb("agg", [P, KD, GROUP], F32)
        side = sb("side", [P, KD, GROUP], F32)
        u = sb("u", [P, GT, D], F32)
        v = sb("v", [P, GT, D], F32)
        w = sb("w", [P, GT, D], F32)
        x_in = w
        colw = sb("colw", [P, CW], F32)
        col = sb("col", [P, GROUP], F32)
        value_rows = sb("value_rows", [P, TILES], F32)
        zero_rows = sb("zero_rows", [P, TILES], F32)
        counts = sb("counts", [P, 2, CHUNKS], F32)
        surplus = sb("surplus", [P, CHUNKS], F32)
        odd_ones = sb("odd_ones", [P, 2], F32)
        odd_sum = sb("odd_sum", [P, 1], F32)
        one_value = sb("one_value", [1, 1], I32)
        w1_s = sb("w1_s", [P, 2 * KD, D], F32)
        w2_s = sb("w2_s", [P, 2 * KD, D], F32)
        wh_s = sb("wh_s", [P, KD, D], F32)
        w2a_s = sb("w2a_s", [P, KD, P], F32)
        w2b_s = sb("w2b_s", [P, D], F32)
        w3_s = sb("w3_s", [P, KD, D], F32)
        b1_s = sb("b1_s", [P, D], F32)
        b2_s = sb("b2_s", [P, D], F32)
        bh_s = sb("bh_s", [P, D], F32)
        b2a_s = sb("b2a_s", [P, P], F32)
        b2b_s = sb("b2b_s", [P, D], F32)
        b3_s = sb("b3_s", [P, D], F32)
        ident = sb("ident", [P, P], F32)
        ident_up = sb("ident_up", [P, P], F16)
        ones = sb("ones", [P, 1], F32)
        ln_eps = sb("ln_eps", [P, 1], F32)
        zero = sb("zero", [P, 1], F32)
        deg = sb("deg", [P, TILES], F32)
        none = sb("none", [P, GT], F32)
        sums = sb("sums", [P, 2, GT], F32)
        root = sb("root", [P, 2, GT], F32)
        root_scrap = sb("root_scrap", [P, 2, GT], F32)
        r_norm = sb("r_norm", [P, TILES], F32)
        r_last = sb("r_last", [P, TILES], F32)
        adj_r = sb("adj_r", [P, TILES], F32)
        stats = sb("stats", [P, GT, 6], F32)
        mv = sb("mv", [P, GT, 2], F32)
        std = sb("std", [P, GT], F32)
        guess = sb("guess", [P, GT], F32)
        scrap = sb("scrap", [P, GT], F32)
        rstd = sb("rstd", [P, GT], F32)

        main = [ps("main0", [P, GROUP]), ps("main1", [P, GROUP])]
        p_turn = ps("p_turn", [P, KD, GROUP])
        p_y = ps("p_y", [P, GT, D])
        p_h = ps("p_h", [P, GT, P])
        p_col = ps("p_col", [P, GROUP])

        masks = nc.dram_tensor("masks", (GROUPS, LOADS, P, PAIR, CW), U8, kind="Internal").ap()

        consts_set = sem("consts_set")
        ident_zero = sem("ident_zero")
        weights_in = sem("weights_in")
        values_in = sem("values_in")
        mask_made = sem("mask_made")
        equal_counted = sem("equal_counted")
        surplus_found = sem("surplus_found")
        surplus_added = sem("surplus_added")
        mask_out = [sem(f"mask_out{i}") for i in range(RAW)]
        mask_in = [sem(f"mask_in{i}") for i in range(LOADS)]
        odd_step = sem("odd_step")
        odd_counted = sem("odd_counted")
        odd_summed = sem("odd_summed")
        one_value_set = sem("one_value_set")
        left = sem("left")

        class Signals:

            def __init__(self, way):
                self.x_piece_in = [sem(f"{way}_x_piece_in{c}") for c in range(CHUNKS)]
                self.raw_in = [sem(f"{way}_raw_in{s}") for s in range(RAW)]
                self.side_in = sem(f"{way}_side_in")
                self.x_again_in = sem(f"{way}_x_again_in")
                self.hi_cut = sem(f"{way}_hi_cut")
                self.lo_cut = sem(f"{way}_lo_cut")
                self.chunk_used = sem(f"{way}_chunk_used")
                self.half0_done = sem(f"{way}_half0_done")
                self.half_out = [sem(f"{way}_half0_out"), sem(f"{way}_half1_out")]
                self.fhi_set = sem(f"{way}_fhi_set")
                self.flo_set = sem(f"{way}_flo_set")
                self.y_done = sem(f"{way}_y_done")
                self.y_read = sem(f"{way}_y_read")
                self.v_set = sem(f"{way}_v_set")
                self.v_part = sem(f"{way}_v_part")
                self.relu_set = sem(f"{way}_relu_set")
                self.u_set = sem(f"{way}_u_set")
                self.turned = sem(f"{way}_turned")
                self.turn_out = [sem(f"{way}_turn0_out"), sem(f"{way}_turn1_out")]
                self.h_done = sem(f"{way}_h_done")
                self.stats_set = sem(f"{way}_stats_set")
                self.mv_set = sem(f"{way}_mv_set")
                self.std_set = sem(f"{way}_std_set")
                self.rstd_set = sem(f"{way}_rstd_set")
                self.x_new = sem(f"{way}_x_new")
                self.x_kept = sem(f"{way}_x_kept")
                self.w_part = sem(f"{way}_w_part")
                self.w_set = sem(f"{way}_w_set")
                self.col_step = sem(f"{way}_col_step")
                self.col_set = sem(f"{way}_col_set")
                self.col_done = sem(f"{way}_col_done")
                self.deg_set = sem(f"{way}_deg_set")
                self.none_set = sem(f"{way}_none_set")
                self.root_in = sem(f"{way}_root_in")
                self.root_set = sem(f"{way}_root_set")
                self.recip_set = sem(f"{way}_recip_set")
                self.r_set = sem(f"{way}_r_set")
                self.adj_r_set = sem(f"{way}_adj_r_set")
                self.extra_set = sem(f"{way}_extra_set")
                self.out_set = sem(f"{way}_out_set")
                self.out_written = sem(f"{way}_out_written")
                self.own_turned = sem(f"{way}_own_turned")
                self.own_out = sem(f"{way}_own_out")
                self.agg_part = sem(f"{way}_agg_part")
                self.agg_set = sem(f"{way}_agg_set")
                self.guess_set = sem(f"{way}_guess_set")
                self.newton = sem(f"{way}_newton")
                self.root_newton = sem(f"{way}_root_newton")
                self.root_exact = sem(f"{way}_root_exact")

        by_mask = Signals("mask")
        by_parts = Signals("parts")

        def tail_of(l, g):
            if is_first(g):
                return l - 1, GROUPS - 1
            return l, g - 1

        def is_first(g):
            return isinstance(g, int) and g == 0

        def free(eng, semaphore, count):
            if not is_first(count):
                eng.wait_ge(semaphore, count)

        def steady(eng, *values):
            held = [v if isinstance(v, int) else eng.snap(eng.to_reg(v)) for v in values]
            eng.wait_ge(consts_set, 1)
            return held

        def rows(t, g):
            return t[:, bass.ds(g * GT, GT)]

        def layer(eng, s, l, group):
            group(s, l, 0)
            group(s, l, 1)
            with eng.Fori(2, GROUPS) as g:
                group(s, l, g)

        def run(eng, group, last, decided, again):
            layer(eng, by_mask, CONV1, group)
            decided()
            eng.wait_ge(one_value_set, 1)
            flag = eng.value_load(one_value[0:1, 0:1], min_val=0, max_val=1)
            with eng.If(flag == 1):
                for l in range(CONV2, LAYERS):
                    layer(eng, by_mask, l, group)
                last(by_mask, LAST, GROUPS - 1)
            with eng.Else():
                eng.drain()
                eng.nop().then_inc(left, 1)
                eng.wait_ge(left, 5)
                again()
                for l in range(LAYERS):
                    layer(eng, by_parts, l, group)
                last(by_parts, LAST, GROUPS - 1)

        def nothing():
            pass

        def summed(s, l, g, c):
            if l == CONV2:
                return s.col_step, g * (CHUNKS + 1) + c + 1
            if l == HEADS and c < CHUNKS - 1:
                return s.col_step, GROUPS * (CHUNKS + 1) + g * (TILES - 1) + (c + 1) * CT
            if l == HEADS:
                return s.col_set, GROUPS + g + 1
            return s.chunk_used, 0

        block = ctx.enter_context(nc.Block())


        @block.gpsimd
        def _(pool):
            nc.gpsimd.memset(ident[:], 0.0)
            nc.gpsimd.memset(ident_up[:], 0.0).then_inc(ident_zero, 1)
            nc.gpsimd.memset(ones[:], 1.0)
            nc.gpsimd.memset(ln_eps[:], LN_EPS)
            nc.gpsimd.memset(zero[:], 0.0).then_inc(consts_set, 1)
            pool.wait_ge(ident_zero, 1)
            nc.gpsimd.affine_select(out=ident[:], in_=ident[:], compare_op=ALU.not_equal, fill=1.0,
                                    base=0, pattern=[[-1, P]], channel_multiplier=1).then_inc(consts_set, 1)
            nc.gpsimd.affine_select(out=ident_up[:], in_=ident_up[:], compare_op=ALU.not_equal, fill=A_UP,
                                    base=0, pattern=[[-1, P]], channel_multiplier=1).then_inc(consts_set, 1)

            pool.wait_ge(one_value_set, 1)
            flag = pool.value_load(one_value[0:1, 0:1], min_val=0, max_val=1)
            with pool.If(flag == 0):
                pool.drain()
                pool.nop().then_inc(left, 1)

        @block.sync
        def _(sp):
            def load_raw(s, l, g, c):
                k = (l * GROUPS + g) * CHUNKS + c
                if s is by_mask and not (is_first(g) and c < RAW):
                    sp.wait_ge(mask_made, k - RAW + 1)
                    sp.wait_ge(equal_counted, k - RAW + 1)
                if s is by_parts and not (l == 0 and is_first(g) and c < RAW):
                    read, count = summed(s, l, g, c - RAW) if c >= RAW else summed(s, *tail_of(l, g), c + CHUNKS - RAW)
                    done, count, g = steady(sp, k - RAW + 1, count, g)
                    sp.wait_ge(s.hi_cut, done)
                    sp.wait_ge(s.lo_cut, done)
                    free(sp, read, count)
                sp.dma_start(raw[:, c % RAW, :], adjT[g, c]).then_inc(s.raw_in[c % RAW], 16)

            def store_mask(g, c):
                made, g = steady(sp, g * CHUNKS + c + 1, g)
                sp.wait_ge(mask_made, made)
                sp.dma_start(masks[g, c // PAIR, :, c % PAIR, :], mask_made_ring[:, c % RAW, :].bitcast(U8)).then_inc(
                    mask_out[c % RAW], 16)

            def load_mask(s, l, g, q):
                tl, tg = tail_of(l, g)
                if tl >= CONV2:
                    read, count = summed(s, tl, tg, (q + 1) * PAIR - 1)
                    used, count, g = steady(sp, (tl * GROUPS + tg) * CHUNKS + (q + 1) * PAIR, count, g)
                    sp.wait_ge(s.chunk_used, used)
                    free(sp, read, count)
                sp.dma_start(mask_in_ring[:, q].bitcast(U8), masks[g, q]).then_inc(mask_in[q], 16)

            def load_side(s, g):
                free(sp, s.y_done, g)
                sp.dma_start(side[:], xT_t[g]).then_inc(s.side_in, 16)

            def load_x_again(s, g):
                free(sp, s.v_set, 0 if is_first(g) else GROUPS + g)
                sp.dma_start(x_in[:], x_t[g]).then_inc(s.x_again_in, 16)

            def store(s, g):
                sp.wait_ge(s.out_set, g + 1)
                sp.dma_start(out_t[g], u[:]).then_inc(s.out_written, 16)

            def tail(s, tl, tg, c):
                if tl == CONV1 and c == 0:
                    load_side(s, tg)
                if tl == CONV2 and c == 0:
                    load_x_again(s, tg)
                if tl == LAST and c == 5:
                    store(s, tg)

            def group(s, l, g):
                first = l == CONV1 and is_first(g)
                for c in range(CHUNKS):
                    if first:
                        sp.dma_start(xs[:, c * GT:(c + 1) * GT, :], x_t[c]).then_inc(s.x_piece_in[c], 16)
                    if s is by_mask and first and c == 0:
                        sp.dma_start(value_cols, diag.partition_broadcast(P)).then_inc(values_in, 16)
                        sp.dma_start(value_rows[:], diagT).then_inc(values_in, 16)
                    if s is by_mask and l == CONV1:
                        if c >= 3:
                            store_mask(g, c - 3)
                        elif not is_first(g):
                            store_mask(g - 1, c + CHUNKS - 3)
                    if s is by_parts or l == CONV1:
                        load_raw(s, l, g, c)
                    elif c % PAIR == 0 and not (l == CONV2 and is_first(g)):
                        load_mask(s, l, g, c // PAIR)
                    if s is by_mask and first and c == 1:
                        for dst, src in ((w1_s, w1), (w2_s, w2), (wh_s, wh), (w2a_s, w2a), (w3_s, w3)):
                            sp.dma_start(dst[:], src.rearrange("(k p) n -> p k n", p=P)).then_inc(weights_in, 16)
                        sp.dma_start(w2b_s[:], w2b).then_inc(weights_in, 16)
                        for dst, src in ((b1_s, b1), (b2_s, b2), (bh_s, bh), (b2a_s, b2a), (b2b_s, b2b), (b3_s, b3)):
                            sp.dma_start(dst[:], src.partition_broadcast(P)).then_inc(weights_in, 16)
                    tail(s, *tail_of(l, g), c)

            def last(s, tl, tg):
                for c in range(CHUNKS):
                    tail(s, tl, tg, c)
                sp.wait_ge(s.out_written, 16 * GROUPS)

            def decided():
                for c in range(CHUNKS - 3, CHUNKS):
                    store_mask(GROUPS - 1, c)
                sp.wait_ge(equal_counted, GROUPS * CHUNKS)
                for i in range(RAW):
                    sp.wait_ge(mask_out[i], 16 * (CHUNKS // RAW))
                for q in range(LOADS):
                    load_mask(by_mask, CONV2, 0, q)
                for i in range(RAW):
                    sp.wait_ge(mask_out[i], 16 * GROUPS * (CHUNKS // RAW))

            def again():
                for q in range(LOADS):
                    sp.wait_ge(mask_in[q], 16)

            run(sp, group, last, decided, again)

        WEIGHTS = 16 * 12

        @block.tensor
        def _(pe):
            def products(s, l, g, c, ready, count, terms):
                buf = l % 2
                count, emptied = steady(pe, count, l * GROUPS + g)
                ready(count)
                pe.wait_ge(s.fhi_set, l * GROUPS + c + 1)
                pe.wait_ge(s.flo_set, l * GROUPS + c + 1)
                for h in range(2):
                    if c == 0 and not (l == CONV1 and is_first(g)):
                        if h == 1:
                            steady(pe)
                        pe.wait_ge(s.half_out[h], emptied)
                    for t in range(CT):
                        m = c * CT + t
                        if l == NORM:
                            at = slice(t * GROUP + h * D, t * GROUP + (h + 1) * D)
                            feat, o = slice(0, P), main[h][:, 0:D]
                        else:
                            at = slice(t * GROUP, (t + 1) * GROUP)
                            feat, o = slice(h * P, (h + 1) * P), main[h][:]
                        for i, (features, chunk) in enumerate(terms):
                            last = nc.tensor.matmul(o, features[:, buf, m, feat], chunk[:, at],
                                                    start=(m == 0 and i == 0),
                                                    stop=(m == TILES - 1 and i == len(terms) - 1
                                                          and not (l == NORM and s is by_parts)))
                    if c == CHUNKS - 1 and l == NORM and s is by_parts:
                        for j in (2 * h, 2 * h + 1):
                            o = main[h][:, (j % 2) * P:(j % 2 + 1) * P]
                            last = own_features(g, j, o, start=False, stop=(j % 2 == 1))
                    if c == CHUNKS - 1 and h == 0:
                        last.then_inc(s.half0_done, 1)
                last.then_inc(s.chunk_used, 1)

            def own_features(g, j, o, start, stop):
                for n, part in enumerate((f_hi, f_lo)):
                    own = part[:, NORM % 2, bass.ds(g * GT + j, 1), 0:P].rearrange("p a b -> p (a b)")
                    last = nc.tensor.matmul(o, own, ident_up[:], start=start and n == 0, stop=stop and n == 1)
                return last

            def stream(s, l, g, c):
                k = (l * GROUPS + g) * CHUNKS + c

                def parts_ready(count):
                    pe.wait_ge(s.hi_cut, count)
                    pe.wait_ge(s.lo_cut, count)

                def made_ready(count):
                    pe.wait_ge(mask_made, count)

                def mask_ready(count):
                    pe.wait_ge(mask_in[c // PAIR], count)

                if s is by_parts:
                    upper, lower = a_hi[:, c % CUT, :], a_lo[:, c % CUT, :]
                    products(s, l, g, c, parts_ready, k + 1, [(f_hi, upper), (f_hi, lower), (f_lo, upper)])
                elif l == CONV1:
                    mask = mask_made_ring[:, c % RAW, :]
                    products(s, l, g, c, made_ready, k + 1, [(f_hi, mask), (f_lo, mask)])
                else:
                    mask = mask_in_ring[:, c // PAIR, c % PAIR, :]
                    products(s, l, g, c, mask_ready, 16 * ((l - CONV2) * GROUPS + g + 1), [(f_hi, mask), (f_lo, mask)])

            def turn_own(s, tg):
                pe.wait_ge(s.turn_out[0], 2 * GROUPS)
                pe.wait_ge(s.turn_out[1], 2 * GROUPS)
                free(pe, s.own_out, tg)
                for j in range(GT):
                    last = own_features(tg, j, p_turn[:, 0, j * P:(j + 1) * P], start=True, stop=True)
                last.then_inc(s.own_turned, 1)

            def turn(s, tl, tg):
                count = (GROUPS if tl == HEADS else 0) + tg + 1
                if tl == CONV2:
                    pe.wait_ge(s.u_set, tg + 1)
                else:
                    pe.wait_ge(s.x_new, count)
                pe.wait_ge(consts_set, 3)
                for h in range(2):
                    free(pe, s.turn_out[h], count - 1)
                for h in range(KD):
                    for j in range(GT):
                        last = nc.tensor.transpose(p_turn[:, h, j * P:(j + 1) * P], u[:, j, h * P:(h + 1) * P], ident[:])
                last.then_inc(s.turned, 1)

            def product(s, tl, tg):
                n = tl * GROUPS + tg
                if s is by_mask:
                    pe.wait_ge(s.agg_set, n + 1)
                else:
                    pe.wait_ge(s.half_out[0], n + 1)
                pe.wait_ge(s.half_out[1], n + 1)
                free(pe, s.v_set, n)
                if tl == CONV1:
                    pe.wait_ge(s.side_in, 16 * (tg + 1))
                    pe.wait_ge(weights_in, WEIGHTS)
                if tl == CONV2:
                    pe.wait_ge(s.turn_out[0], tg + 1)
                    pe.wait_ge(s.turn_out[1], tg + 1)
                parts = {CONV1: [(side, 0, w1_s[:, 0]), (side, 1, w1_s[:, 1]), (agg, 0, w1_s[:, 2]), (agg, 1, w1_s[:, 3])],
                         CONV2: [(side, 0, w2_s[:, 0]), (side, 1, w2_s[:, 1]), (agg, 0, w2_s[:, 2]), (agg, 1, w2_s[:, 3])],
                         HEADS: [(agg, 0, wh_s[:, 0]), (agg, 1, wh_s[:, 1])],
                         NORM: [(agg, 0, w2b_s[:])],
                         LAST: [(agg, 0, w3_s[:, 0]), (agg, 1, w3_s[:, 1])]}[tl]
                for j in range(GT):
                    for i, (t, k, wt) in enumerate(parts):
                        last = nc.tensor.matmul(p_y[:, j, :], t[:, k, j * P:(j + 1) * P], wt,
                                                start=(i == 0), stop=(i == len(parts) - 1))
                last.then_inc(s.y_done, 1)

            def hidden(s, tg):
                pe.wait_ge(s.turn_out[0], GROUPS + tg + 1)
                pe.wait_ge(s.turn_out[1], GROUPS + tg + 1)
                free(pe, s.w_part, tg)
                for j in range(GT):
                    for k in range(KD):
                        last = nc.tensor.matmul(p_h[:, j, :], side[:, k, j * P:(j + 1) * P], w2a_s[:, k],
                                                start=(k == 0), stop=(k == KD - 1))
                last.then_inc(s.h_done, 1)

            def columns(s, tl, tg):
                n = (tl - CONV2) * GROUPS + tg
                pe.wait_ge(s.col_set, n + 1)
                if is_first(n):
                    pe.wait_ge(consts_set, 1)
                free(pe, s.deg_set, tg if tl == CONV2 else GROUPS)
                if tl == HEADS:
                    free(pe, s.adj_r_set, tg)
                for j in range(GT):
                    last = nc.tensor.matmul(p_col[:, j:j + 1], col[:, j * P:(j + 1) * P], ones[:], start=True, stop=True)
                last.then_inc(s.col_done, 1)

            def tail(s, tl, tg, c):
                if tl in (CONV2, HEADS) and c == 0:
                    columns(s, tl, tg)
                if tl == CONV2 and c == 0:
                    turn(s, tl, tg)
                if tl == NORM and s is by_mask and c == 0:
                    turn_own(s, tg)
                if tl >= 0 and c == (2 if tl == CONV2 else 1):
                    product(s, tl, tg)
                if tl == HEADS and c == 4:
                    turn(s, tl, tg)
                if tl == HEADS and c == 5:
                    hidden(s, tg)

            def group(s, l, g):
                for c in range(CHUNKS):
                    stream(s, l, g, c)
                    tail(s, *tail_of(l, g), c)

            def last(s, tl, tg):
                for c in range(CHUNKS):
                    tail(s, tl, tg, c)

            def decided():
                pe.wait_ge(odd_counted, 1)
                nc.tensor.matmul(p_h[0:1, 0, 0:2], ones[:], odd_ones[:], start=True, stop=True).then_inc(odd_summed, 1)

            run(pe, group, last, decided, nothing)

        @block.scalar
        def _(act):
            def first_features(s, c):
                act.wait_ge(s.x_piece_in[c], 16)
                nc.scalar.activation(f_hi[:, 0, c * GT:(c + 1) * GT, :], xs[:, c * GT:(c + 1) * GT, :], ACT.Copy,
                                     scale=F_UP).then_inc(s.fhi_set, 1)

            def stream(s, l, g, c):
                k = (l * GROUPS + g) * CHUNKS + c
                came = 16 * ((l * GROUPS + g) * (CHUNKS // RAW) + c // RAW + 1)
                if s is by_parts:
                    act.wait_ge(s.raw_in[c % RAW], came)
                    if not (l == 0 and is_first(g) and c < CUT):
                        act.wait_ge(s.chunk_used, k - CUT + 1)
                    nc.scalar.activation(a_hi[:, c % CUT, :], raw[:, c % RAW, :], ACT.Copy, scale=A_UP).then_inc(s.hi_cut, 1)
                elif l == CONV1:
                    came, used, written, read = steady(act, came, k - RAW + 1, 16 * (g * (CHUNKS // RAW) + c // RAW), g)
                    act.wait_ge(s.raw_in[c % RAW], came)
                    if not (is_first(g) and c < RAW):
                        act.wait_ge(s.chunk_used, used)
                        act.wait_ge(mask_out[c % RAW], written)
                    if c == 0:
                        free(act, surplus_added, read)
                    nc.scalar.activation(mask_made_ring[:, c % RAW, :], raw[:, c % RAW, :].bitcast(U32), ACT.Sign,
                                         saturate=False, accum_out=counts[:, 0, c:c + 1]).then_inc(mask_made, 1)

            def tail(s, tl, tg, c):
                if tl < 0:
                    return
                n = tl * GROUPS + tg
                if c == 0:
                    if tl == CONV2:
                        free(act, s.turned, tg)
                        nc.scalar.activation(u[:], rows(xs, tg), ACT.Copy).then_inc(s.u_set, 1)
                    act.wait_ge(s.half0_done, n + 1)
                    free(act, s.y_done, n)
                    wide = D if tl == NORM else GROUP
                    nc.scalar.activation(agg[:, 0, 0:wide], main[0][:, 0:wide], ACT.Copy,
                                         scale=1 / F_UP if s is by_mask else DOWN).then_inc(s.half_out[0], 1)
                    if tl == NORM and s is by_mask:
                        act.wait_ge(s.own_turned, tg + 1)
                        act.wait_ge(s.h_done, GROUPS)
                        act.wait_ge(s.agg_set, n)
                        nc.scalar.activation(side[:, 0, :], p_turn[:, 0, :], ACT.Copy, scale=DOWN).then_inc(s.own_out, 1)
                if (tl == CONV2 and c == 1) or (tl == HEADS and c == 4):
                    count = (GROUPS if tl == HEADS else 0) + tg + 1
                    act.wait_ge(s.turned, count)
                    if tl == HEADS:
                        free(act, s.h_done, tg)
                    nc.scalar.activation(side[:, 0, :], p_turn[:, 0, :], ACT.Copy).then_inc(s.turn_out[0], 1)
                if tl == CONV1 and c == 2:
                    act.wait_ge(s.v_set, n + 1)
                    nc.scalar.activation(rows(xs, tg), v[:], ACT.Relu).then_inc(s.relu_set, 1)
                    nc.scalar.activation(f_hi[:, 1, bass.ds(tg * GT, GT), :], v[:], ACT.Relu, scale=F_UP).then_inc(s.fhi_set, 1)
                if tl in (CONV2, HEADS, NORM, LAST) and c == (3 if tl == CONV2 else 2):
                    act.wait_ge(s.mv_set, (tl - CONV2) * GROUPS + tg + 1)
                    nc.scalar.activation(std[:], mv[:, :, 1:2].rearrange("p a b -> p (a b)"), ACT.Sqrt,
                                         bias=ln_eps[:]).then_inc(s.std_set, 1)
                if tl == CONV2 and c == 4:
                    act.wait_ge(s.x_new, tg + 1)
                    nc.scalar.activation(f_hi[:, 0, bass.ds(tg * GT, GT), :], rows(xs, tg), ACT.Copy,
                                         scale=F_UP).then_inc(s.fhi_set, 1)
                if tl in (HEADS, NORM) and c == 3:
                    act.wait_ge(s.x_new, (tl - CONV2) * GROUPS + tg + 1)
                    nc.scalar.activation(rows(xs, tg), u[:], ACT.Copy).then_inc(s.x_kept, 1)
                if tl in (HEADS, NORM) and c == (5 if tl == HEADS else 4):
                    act.wait_ge(s.w_set, (tl - HEADS) * GROUPS + tg + 1)
                    wide = P if tl == HEADS else D
                    nc.scalar.activation(f_hi[:, (tl + 1) % 2, bass.ds(tg * GT, GT), 0:wide], w[:, :, 0:wide], ACT.Copy,
                                         scale=F_UP).then_inc(s.fhi_set, 1)
                if tl == CONV2 and c == 2:
                    act.wait_ge(s.root_in, tg + 1)
                    nc.scalar.activation(root[:], sums[:], ACT.Sqrt, bias=zero[:]).then_inc(s.root_set, 1)

            def group(s, l, g):
                if l == CONV1 and is_first(g):
                    act.wait_ge(consts_set, 1)
                for c in range(CHUNKS):
                    if l == CONV1 and is_first(g):
                        first_features(s, c)
                    stream(s, l, g, c)
                    tail(s, *tail_of(l, g), c)

            def last(s, tl, tg):
                for c in range(CHUNKS):
                    tail(s, tl, tg, c)

            run(act, group, last, nothing, nothing)

        @block.vector
        def _(dve):
            def cut_low(dst, src, upper, up):
                return nc.vector.scalar_tensor_tensor(out=dst, in0=src, scalar=up, in1=upper,
                                                      op0=ALU.mult, op1=ALU.subtract)

            def first_features(s, c):
                at = slice(c * GT, (c + 1) * GT)
                dve.wait_ge(s.x_piece_in[c], 16)
                dve.wait_ge(s.fhi_set, c + 1)
                cut_low(f_lo[:, 0, at, :].rearrange("p a b -> p (a b)"), xs[:, at, :].rearrange("p a b -> p (a b)"),
                        f_hi[:, 0, at, :].rearrange("p a b -> p (a b)"), F_UP).then_inc(s.flo_set, 1)

            def stream(s, l, g, c):
                k = (l * GROUPS + g) * CHUNKS + c
                came = 0
                if s is by_parts:
                    chunk = raw[:, c % RAW, :]
                    dve.wait_ge(s.raw_in[c % RAW], 16 * ((l * GROUPS + g) * (CHUNKS // RAW) + c // RAW + 1))
                    dve.wait_ge(s.hi_cut, k + 1)
                    if not (l == 0 and is_first(g) and c < CUT):
                        dve.wait_ge(s.chunk_used, k - CUT + 1)
                    cut_low(a_lo[:, c % CUT, :], chunk, a_hi[:, c % CUT, :], A_UP).then_inc(s.lo_cut, 1)
                elif l == CONV1:
                    chunk = raw[:, c % RAW, :].rearrange("p (t n) -> p t n", t=CT)
                    values = value_cols[:, bass.ds(g * GROUP, GROUP)].unsqueeze(1).to_broadcast([P, CT, GROUP])
                    scrap = colw[:, 0:CW // 2].bitcast(BF16).rearrange("p (t n) -> p t n", t=CT)
                    dve.wait_ge(s.raw_in[c % RAW], 16 * (g * (CHUNKS // RAW) + c // RAW + 1))
                    free(dve, equal_counted, k)
                    if c == 0:
                        free(dve, surplus_added, g)
                    nc.vector.scalar_tensor_tensor(out=scrap, in0=chunk, scalar=1.0, in1=values, op0=ALU.mult,
                                                   op1=ALU.is_equal,
                                                   accum_out=counts[:, 1, c:c + 1],
                                                   ).then_inc(equal_counted, 1)
                    if c == CHUNKS - 1:
                        dve.wait_ge(equal_counted, k + 1)
                        dve.wait_ge(mask_made, k + 1)
                        if is_first(g):
                            nc.vector.tensor_tensor(surplus[:], counts[:, 0, :], counts[:, 1, :], ALU.subtract).then_inc(surplus_added, 1)
                        else:
                            nc.vector.tensor_tensor(counts[:, 0, :], counts[:, 0, :], counts[:, 1, :], ALU.subtract).then_inc(surplus_found, 1)
                            dve.wait_ge(surplus_found, g)
                            nc.vector.tensor_tensor(surplus[:], surplus[:], counts[:, 0, :], ALU.add).then_inc(surplus_added, 1)
                else:
                    chunk = mask_in_ring[:, c // PAIR, c % PAIR, :]
                    came = 16 * ((l - CONV2) * GROUPS + g + 1)
                if l == CONV2:
                    n = g * (CHUNKS + 1)
                    if c == 0:
                        came, read = steady(dve, came, g) if s is by_mask else (came, g)
                        if s is by_mask:
                            dve.wait_ge(mask_in[c // PAIR], came)
                        free(dve, s.col_set, read)
                        nc.vector.tensor_copy(colw[:], chunk).then_inc(s.col_step, 1)
                    else:
                        came, before = steady(dve, came, n + c) if s is by_mask else (came, n + c)
                        if s is by_mask:
                            dve.wait_ge(mask_in[c // PAIR], came)
                        dve.wait_ge(s.col_step, before)
                        nc.vector.tensor_tensor(colw[:], colw[:], chunk, ALU.add).then_inc(s.col_step, 1)
                    if c == CHUNKS - 1:
                        dve.wait_ge(s.col_step, n + CHUNKS)
                        nc.vector.tensor_tensor(colw[:, 0:2 * GROUP], colw[:, 0:2 * GROUP], colw[:, 2 * GROUP:],
                                                ALU.add).then_inc(s.col_step, 1)
                        dve.wait_ge(s.col_step, n + CHUNKS + 1)
                        free(dve, s.col_done, g)
                        nc.vector.tensor_tensor(col[:], colw[:, 0:GROUP], colw[:, GROUP:2 * GROUP],
                                                ALU.add).then_inc(s.col_set, 1)
                if l == HEADS:
                    n = GROUPS * (CHUNKS + 1) + g * (TILES - 1)
                    dve.wait_ge(s.r_set, c + 1 if is_first(g) else GROUPS)
                    for t in range(CT):
                        m = c * CT + t
                        part = chunk[:, t * GROUP:(t + 1) * GROUP]
                        r = r_norm[:, m:m + 1]
                        came, before, read = steady(dve, came, n + m, GROUPS + g) if s is by_mask else (came, n + m, GROUPS + g)
                        if s is by_mask and t == 0:
                            dve.wait_ge(mask_in[c // PAIR], came)
                        if m == 0:
                            dve.wait_ge(s.col_set, read)
                            nc.vector.tensor_scalar(colw[:, 0:GROUP], part, r, None, ALU.mult).then_inc(s.col_step, 1)
                        elif m < TILES - 1:
                            dve.wait_ge(s.col_step, before)
                            nc.vector.scalar_tensor_tensor(out=colw[:, 0:GROUP], in0=part, scalar=r, in1=colw[:, 0:GROUP],
                                                           op0=ALU.mult, op1=ALU.add).then_inc(s.col_step, 1)
                        else:
                            dve.wait_ge(s.col_step, before)
                            dve.wait_ge(s.col_done, read)
                            nc.vector.scalar_tensor_tensor(out=col[:], in0=part, scalar=r, in1=colw[:, 0:GROUP],
                                                           op0=ALU.mult, op1=ALU.add).then_inc(s.col_set, 1)

            def bias(t):
                return t[:].unsqueeze(1).to_broadcast([P, GT, t.shape[1]])

            def inverse_root(dst, value, eps, guess, scrap, step, n, done):
                nc.vector.scalar_tensor_tensor(out=scrap, in0=value, scalar=eps, in1=guess, op0=ALU.add,
                                               op1=ALU.mult).then_inc(step, 1)
                dve.wait_ge(step, 2 * n + 1)
                nc.vector.scalar_tensor_tensor(out=scrap, in0=scrap, scalar=-0.5, in1=guess, op0=ALU.mult,
                                               op1=ALU.mult).then_inc(step, 1)
                dve.wait_ge(step, 2 * n + 2)
                nc.vector.scalar_tensor_tensor(out=dst, in0=scrap, scalar=1.5, in1=guess, op0=ALU.add,
                                               op1=ALU.mult).then_inc(done, 1)

            def norm(s, tl, tg, dst):
                n = (tl - CONV2) * GROUPS + tg
                dve.wait_ge(s.v_set, tl * GROUPS + tg + 1)
                for j in range(GT):
                    last = nc.vector.bn_stats(stats[:, j, :], v[:, j, :])
                last.then_inc(s.stats_set, 1)
                steady(dve)
                dve.wait_ge(s.stats_set, n + 1)
                for j in range(GT):
                    last = nc.vector.bn_aggr(mv[:, j, :], stats[:, j, :])
                last.then_inc(s.mv_set, 1)
                dve.wait_ge(s.std_set, n + 1)
                nc.vector.reciprocal(guess[:], std[:]).then_inc(s.guess_set, 1)
                dve.wait_ge(s.guess_set, n + 1)
                inverse_root(rstd[:].unsqueeze(2), mv[:, :, 1:2], LN_EPS, guess[:].unsqueeze(2), scrap[:].unsqueeze(2),
                             s.newton, n, s.rstd_set)
                dve.wait_ge(s.rstd_set, n + 1)
                for j in range(GT):
                    last = nc.vector.tensor_scalar(dst(j), v[:, j, :], mv[:, j, 0:1], rstd[:, j:j + 1],
                                                   ALU.subtract, ALU.mult)
                return last

            def cut_w(s, tl, tg):
                wide = P if tl == HEADS else D
                dve.wait_ge(s.fhi_set, (tl + 1) * GROUPS + tg + 1)
                nc.vector.scalar_tensor_tensor(out=f_lo[:, (tl + 1) % 2, bass.ds(tg * GT, GT), 0:wide],
                                               in0=w[:, :, 0:wide], scalar=F_UP,
                                               in1=f_hi[:, (tl + 1) % 2, bass.ds(tg * GT, GT), 0:wide],
                                               op0=ALU.mult, op1=ALU.subtract).then_inc(s.flo_set, 1)

            def tail(s, tl, tg, c):
                if tl < 0:
                    return
                n = tl * GROUPS + tg
                if c == 0:
                    dve.wait_ge(s.chunk_used, CHUNKS * (n + 1))
                    free(dve, s.y_done, n)
                    wide = D if tl == NORM else GROUP
                    second = agg[:, 0, D:2 * D] if tl == NORM else agg[:, 1, :]
                    if s is by_parts:
                        nc.vector.tensor_scalar(second, main[1][:, 0:wide], DOWN, None, ALU.mult).then_inc(s.half_out[1], 1)
                    else:
                        value = value_cols[:, bass.ds(tg * GROUP, wide)]
                        value2 = value_cols[:, bass.ds(tg * GROUP + (D if tl == NORM else 0), wide)]
                        nc.vector.scalar_tensor_tensor(out=second, in0=main[1][:, 0:wide], scalar=1 / F_UP, in1=value2,
                                                       op0=ALU.mult, op1=ALU.mult).then_inc(s.half_out[1], 1)
                        dve.wait_ge(s.half_out[0], n + 1)
                        scaled = nc.vector.tensor_tensor(agg[:, 0, 0:wide], agg[:, 0, 0:wide], value, ALU.mult)
                        if tl != NORM:
                            scaled.then_inc(s.agg_set, 1)
                        else:
                            scaled.then_inc(s.agg_part, 1)
                            dve.wait_ge(s.agg_part, tg + 1)
                            dve.wait_ge(s.own_out, tg + 1)
                            nc.vector.tensor_tensor(agg[:, 0, :], agg[:, 0, :], side[:, 0, :], ALU.add).then_inc(s.agg_set, 1)
                if (tl == CONV2 and c == 1) or (tl == HEADS and c == 4):
                    count = (GROUPS if tl == HEADS else 0) + tg + 1
                    dve.wait_ge(s.turned, count)
                    if tl == HEADS:
                        free(dve, s.h_done, tg)
                    nc.vector.tensor_copy(side[:, 1, :], p_turn[:, 1, :]).then_inc(s.turn_out[1], 1)
                if tl == CONV2 and c == 1:
                    dve.wait_ge(s.col_done, tg + 1)
                    if s is by_mask:
                        nc.vector.tensor_tensor(rows(deg, tg), p_col[:, 0:GT], rows(value_rows, tg), ALU.mult).then_inc(s.deg_set, 1)
                    else:
                        nc.vector.tensor_copy(rows(deg, tg), p_col[:, 0:GT]).then_inc(s.deg_set, 1)
                    dve.wait_ge(s.deg_set, tg + 1)
                    free(dve, s.r_set, tg)
                    nc.vector.tensor_scalar(none[:], rows(deg, tg), 1.0, 0.0, ALU.add, ALU.is_equal).then_inc(s.none_set, 1)
                    nc.vector.tensor_scalar(sums[:, 1, :], rows(deg, tg), DEG_EPS, None, ALU.add)
                    dve.wait_ge(s.none_set, 2 * tg + 1)
                    nc.vector.scalar_tensor_tensor(out=sums[:, 0, :], in0=rows(deg, tg), scalar=1.0, in1=none[:],
                                                   op0=ALU.add, op1=ALU.add).then_inc(s.root_in, 1)
                if tl == CONV2 and c == 2:
                    dve.wait_ge(s.root_set, tg + 1)
                    nc.vector.reciprocal(root[:], root[:]).then_inc(s.recip_set, 1)
                    nc.vector.tensor_scalar(none[:], none[:], -1.0, 1.0, ALU.mult, ALU.add).then_inc(s.none_set, 1)
                    dve.wait_ge(s.recip_set, tg + 1)
                    inverse_root(root[:], sums[:], 0.0, root[:], root_scrap[:], s.root_newton, tg, s.root_exact)
                    dve.wait_ge(s.none_set, 2 * tg + 2)
                    dve.wait_ge(s.root_exact, tg + 1)
                    nc.vector.tensor_copy(rows(r_last, tg), root[:, 1, :])
                    nc.vector.tensor_tensor(rows(r_norm, tg), root[:, 0, :], none[:], ALU.mult).then_inc(s.r_set, 1)
                if tl == HEADS and c == 1:
                    dve.wait_ge(s.col_done, GROUPS + tg + 1)
                    if s is by_mask:
                        nc.vector.tensor_tensor(rows(adj_r, tg), p_col[:, 0:GT], rows(value_rows, tg), ALU.mult).then_inc(s.adj_r_set, 1)
                    else:
                        nc.vector.tensor_copy(rows(adj_r, tg), p_col[:, 0:GT]).then_inc(s.adj_r_set, 1)
                if tl == CONV1 and c == 2:
                    dve.wait_ge(s.y_done, n + 1)
                    free(dve, s.fhi_set, GROUPS + tg)
                    free(dve, s.relu_set, tg)
                    nc.vector.tensor_tensor(v[:], p_y[:], bias(b1_s), ALU.add).then_inc(s.v_set, 1)
                if tl == CONV1 and c == 3:
                    dve.wait_ge(s.relu_set, tg + 1)
                    dve.wait_ge(s.fhi_set, GROUPS + tg + 1)
                    at = bass.ds(tg * GT, GT)
                    cut_low(f_lo[:, 1, at, :], xs[:, at, :], f_hi[:, 1, at, :], F_UP).then_inc(s.flo_set, 1)
                if tl == CONV2 and c == 3:
                    dve.wait_ge(s.y_done, n + 1)
                    nc.vector.tensor_tensor(v[:], p_y[:], bias(b2_s), ALU.add).then_inc(s.y_read, 1)
                    dve.wait_ge(s.y_read, n - GROUPS + 1)
                    nc.vector.scalar_tensor_tensor(out=v[:], in0=v[:], scalar=0.0, in1=rows(xs, tg), op0=ALU.max,
                                                   op1=ALU.add).then_inc(s.v_part, 1)
                    dve.wait_ge(s.v_part, tg + 1)
                    dve.wait_ge(s.x_again_in, 16 * (tg + 1))
                    nc.vector.scalar_tensor_tensor(out=v[:], in0=v[:], scalar=0.0, in1=x_in[:], op0=ALU.max,
                                                   op1=ALU.add).then_inc(s.v_set, 1)
                    norm(s, tl, tg, lambda j: xs[:, bass.ds(tg * GT + j, 1), :].rearrange("p a b -> p (a b)")).then_inc(s.x_new, 1)
                if tl == CONV2 and c == 4:
                    dve.wait_ge(s.fhi_set, 2 * GROUPS + tg + 1)
                    at = bass.ds(tg * GT, GT)
                    cut_low(f_lo[:, 0, at, :], xs[:, at, :], f_hi[:, 0, at, :], F_UP).then_inc(s.flo_set, 1)
                if tl == HEADS and c == 2:
                    dve.wait_ge(s.y_done, n + 1)
                    nc.vector.tensor_tensor(v[:], p_y[:], bias(bh_s), ALU.add).then_inc(s.y_read, 1)
                    dve.wait_ge(s.y_read, n - GROUPS + 1)
                    nc.vector.tensor_tensor(v[:], v[:], rows(xs, tg), ALU.add).then_inc(s.v_set, 1)
                    dve.wait_ge(s.turned, GROUPS + tg)
                    free(dve, s.x_kept, tg)
                    norm(s, tl, tg, lambda j: u[:, j, :]).then_inc(s.x_new, 1)
                if tl == HEADS and c == 5:
                    dve.wait_ge(s.h_done, tg + 1)
                    dve.wait_ge(s.fhi_set, 3 * GROUPS + tg)
                    dve.wait_ge(s.flo_set, 3 * GROUPS + tg)
                    nc.vector.tensor_tensor(w[:, :, 0:P], p_h[:], bias(b2a_s), ALU.add).then_inc(s.w_part, 1)
                    dve.wait_ge(s.w_part, tg + 1)
                    nc.vector.tensor_tensor(w[:, :, 0:P], w[:, :, 0:P],
                                            rows(r_norm, tg).unsqueeze(2).to_broadcast([P, GT, P]),
                                            ALU.mult).then_inc(s.w_set, 1)
                    cut_w(s, tl, tg)
                if tl == NORM and c == 2:
                    dve.wait_ge(s.y_done, n + 1)
                    nc.vector.tensor_tensor(none[:], rows(adj_r, tg), rows(r_norm, tg), ALU.add).then_inc(s.extra_set, 1)
                    dve.wait_ge(s.extra_set, 2 * tg + 1)
                    for j in range(GT):
                        last = nc.vector.scalar_tensor_tensor(out=v[:, j, :], in0=b2b_s[:], scalar=none[:, j:j + 1],
                                                              in1=p_y[:, j, :], op0=ALU.mult, op1=ALU.add)
                    last.then_inc(s.y_read, 1)
                    dve.wait_ge(s.y_read, n - GROUPS + 1)
                    nc.vector.tensor_tensor(v[:], v[:], rows(r_norm, tg).unsqueeze(2).to_broadcast([P, GT, D]),
                                            ALU.mult).then_inc(s.extra_set, 1)
                    dve.wait_ge(s.extra_set, 2 * tg + 2)
                    nc.vector.tensor_tensor(v[:], v[:], rows(xs, tg), ALU.add).then_inc(s.v_set, 1)
                    dve.wait_ge(s.x_kept, GROUPS + tg)
                    norm(s, tl, tg, lambda j: u[:, j, :]).then_inc(s.x_new, 1)
                    dve.wait_ge(s.x_new, 2 * GROUPS + tg + 1)
                    dve.wait_ge(s.fhi_set, 4 * GROUPS + tg)
                    dve.wait_ge(s.flo_set, 4 * GROUPS + tg)
                    nc.vector.tensor_tensor(w[:], u[:], rows(r_last, tg).unsqueeze(2).to_broadcast([P, GT, D]),
                                            ALU.mult).then_inc(s.w_set, 1)
                if tl == NORM and c == 3:
                    dve.wait_ge(s.w_set, GROUPS + tg + 1)
                    cut_w(s, tl, tg)
                if tl == LAST and c == 2:
                    dve.wait_ge(s.y_done, n + 1)
                    free(dve, s.out_set, tg)
                    nc.vector.tensor_tensor(v[:], p_y[:], rows(r_last, tg).unsqueeze(2).to_broadcast([P, GT, D]),
                                            ALU.mult).then_inc(s.y_read, 1)
                    dve.wait_ge(s.y_read, n - GROUPS + 1)
                    nc.vector.tensor_tensor(v[:], v[:], bias(b3_s), ALU.add).then_inc(s.v_part, 1)
                    dve.wait_ge(s.v_part, GROUPS + tg + 1)
                    nc.vector.tensor_tensor(v[:], v[:], rows(xs, tg), ALU.add).then_inc(s.v_set, 1)
                    dve.wait_ge(s.x_kept, 2 * GROUPS)
                    free(dve, s.out_written, 16 * tg)
                    norm(s, tl, tg, lambda j: u[:, j, :]).then_inc(s.out_set, 1)

            def group(s, l, g):
                for c in range(CHUNKS):
                    if l == CONV1 and is_first(g):
                        first_features(s, c)
                    if s is by_mask and l == CONV1 and is_first(g) and c == 0:
                        dve.wait_ge(values_in, 32)
                    stream(s, l, g, c)
                    tail(s, *tail_of(l, g), c)

            def last(s, tl, tg):
                for c in range(CHUNKS):
                    tail(s, tl, tg, c)

            def decided():
                dve.wait_ge(surplus_added, GROUPS)
                nc.vector.tensor_scalar(zero_rows[:], value_rows[:], 0.0, None, ALU.is_equal).then_inc(odd_step, 1)
                dve.wait_ge(odd_step, 1)
                nc.vector.tensor_reduce(odd_ones[:, 0:1], surplus[:], AXX, ALU.add)
                nc.vector.tensor_reduce(odd_ones[:, 1:2], zero_rows[:], AXX, ALU.add).then_inc(odd_counted, 1)
                dve.wait_ge(odd_summed, 1)
                nc.vector.tensor_reduce(odd_sum[0:1, :], p_h[0:1, 0, 0:2], AXX, ALU.add).then_inc(odd_step, 1)
                dve.wait_ge(odd_step, 2)
                nc.vector.tensor_scalar(one_value[:], odd_sum[0:1, :], 0.0, None, ALU.is_equal).then_inc(one_value_set, 1)

            run(dve, group, last, decided, nothing)


_INS = ["x", "xT", "adjT", "diag", "diagT", "w1", "w2", "wh", "w2a", "w2b", "w3", "b1", "b2", "bh", "b2a", "b2b", "b3"]


def kernel(x, adj, L0_gnn_W1, L0_gnn_b1, L0_gnn_W2, L0_gnn_b2, L1_gnn_W, L1_gnn_b, L2_gnn_W1, L2_gnn_b1,
           L2_gnn_W2, L2_gnn_b2, L3_gnn_W, L3_gnn_b):
    import numpy as np
    import concourse.bacc as bacc
    from concourse.bass_utils import run_bass_kernel_spmd

    x, adj = np.asarray(x), np.asarray(adj)
    heads = np.asarray(L1_gnn_W)
    data = {
        "x": x,
        "xT": x.T,
        "adjT": adj.reshape(GROUPS, GROUP, CHUNKS, CT, P).transpose(0, 2, 4, 3, 1).reshape(GROUPS, CHUNKS, P, CW),
        "diag": np.diagonal(adj),
        "diagT": np.diagonal(adj).reshape(TILES, P).T,
        "w1": np.asarray(L0_gnn_W1),
        "w2": np.asarray(L0_gnn_W2),
        "wh": heads.transpose(1, 0, 2).reshape(D, D),
        "w2a": np.asarray(L2_gnn_W1).T,
        "w2b": np.asarray(L2_gnn_W2).T,
        "w3": np.asarray(L3_gnn_W).T,
        "b1": np.asarray(L0_gnn_b1),
        "b2": np.asarray(L0_gnn_b2),
        "bh": np.asarray(L1_gnn_b).reshape(D),
        "b2a": np.asarray(L2_gnn_b1),
        "b2b": np.asarray(L2_gnn_b2),
        "b3": np.asarray(L3_gnn_b),
    }
    nc = bacc.Bacc("TRN2", target_bir_lowering=False, num_devices=1)
    arrays, args = {}, []
    for name in _INS:
        a = np.ascontiguousarray(data[name])
        arrays[f"in_{name}"] = a
        args.append(nc.dram_tensor(f"in_{name}", a.shape, mybir.dt.from_np(a.dtype), kind="ExternalInput").ap())
    args.append(nc.dram_tensor("out", (N, D), F32, kind="ExternalOutput").ap())
    gnn_kernel(nc, *args)
    r = run_bass_kernel_spmd(nc, [arrays], core_ids=[0])
    return r.results[0]["out"]
```

```python
from contextlib import ExitStack

import concourse.bass as bass
from concourse import mybir

F32 = mybir.dt.float32
F16 = mybir.dt.float16
F8 = mybir.dt.float8e4
U32 = mybir.dt.uint32
U8 = mybir.dt.uint8
BF16 = mybir.dt.bfloat16
I32 = mybir.dt.int32
ALU = mybir.AluOpType
ACT = mybir.ActivationFunctionType
AXX = mybir.AxisListType.X

P = 128
N = 4096
D = 256
TILES = N // P
GROUP = 512
GROUPS = N // GROUP
GT = GROUP // P
CT = 4
CHUNKS = TILES // CT
CW = CT * GROUP
GD = GT * D
KD = D // P
RAW = 4
CUT = 2
A_UP = 4096.0
F_UP = 64.0
W_UP = 1024.0
DOWN = 1.0 / (F_UP * W_UP)
LN_EPS = 1e-5
DEG_EPS = 1e-8
PAIR = 2
LOADS = CHUNKS // PAIR
CONV1, CONV2, HEADS, NORM, LAST = range(5)
LAYERS = 5


def gnn_kernel(nc, x, xT, adjT, diag, diagT, w1, w2, wh, w2a, w2b, w3, b1, b2, bh, b2a, b2b, b3, out):
    x_t = x.rearrange("(g j p) d -> g p j d", p=P, j=GT)
    xT_t = xT.rearrange("(k p) (g n) -> g p k n", p=P, n=GROUP)
    out_t = out.rearrange("(g j p) d -> g p j d", p=P, j=GT)

    with ExitStack() as ctx:
        def sb(name, shape, dt):
            return ctx.enter_context(nc.sbuf_tensor(name, shape, dt))

        def ps(name, shape):
            return ctx.enter_context(nc.psum_tensor(name, shape, F32))

        def sem(name):
            return ctx.enter_context(nc.semaphore(name))

        raw = sb("raw", [P, RAW, CW], F32)
        mask_in_ring = raw[:, 0:2, :].rearrange("p s c -> p (s c)").bitcast(F8).rearrange(
            "p (q i c) -> p q i c", q=LOADS, i=PAIR)
        mask_made_ring = sb("mask_made_ring", [P, RAW, CW], F8)
        cut = sb("cut", [P, 2, CUT, CW], F16)
        a_hi, a_lo = cut[:, 0], cut[:, 1]
        value_cols = cut[:, :].rearrange("p a b c -> p (a b c)").bitcast(F32)
        xs = sb("xs", [P, TILES, D], F32)
        f_hi = sb("f_hi", [P, 2, TILES, D], F16)
        f_lo = sb("f_lo", [P, 2, TILES, D], F16)
        agg = sb("agg", [P, KD, GROUP], F32)
        agg_hi = sb("agg_hi", [P, KD, GROUP], F16)
        agg_lo = sb("agg_lo", [P, KD, GROUP], F16)
        side = sb("side", [P, KD, GROUP], F32)
        side_hi = side[:, 0, :].bitcast(F16).rearrange("p (k n) -> p k n", k=KD)
        side_lo = side[:, 1, :].bitcast(F16).rearrange("p (k n) -> p k n", k=KD)
        u = sb("u", [P, GT, D], F32)
        v = sb("v", [P, GT, D], F32)
        w = sb("w", [P, GT, D], F32)
        x_in = w
        colw = sb("colw", [P, CW], F32)
        col = sb("col", [P, GROUP], F32)
        value_rows = sb("value_rows", [P, TILES], F32)
        odd_ones = sb("odd_ones", [P, 2], F32)
        odd_sum = sb("odd_sum", [P, 1], F32)
        one_value = sb("one_value", [1, 1], I32)
        w1_s = sb("w1_s", [P, 2, 2 * KD, D], F16)
        w2_s = sb("w2_s", [P, 2, 2 * KD, D], F16)
        wh_s = sb("wh_s", [P, 2, KD, D], F16)
        w2a_s = sb("w2a_s", [P, 2, KD, P], F16)
        w2b_s = sb("w2b_s", [P, 2, 1, D], F16)
        w3_s = sb("w3_s", [P, 2, KD, D], F16)
        staged = [(v[:].rearrange("p a b -> p (a b)"), w1_s), (u[:].rearrange("p a b -> p (a b)"), w2_s),
                  (colw[:, CW // 2:CW // 2 + KD * D], wh_s), (colw[:, CW // 2 + KD * D:CW // 2 + KD * D + D], w2a_s),
                  (colw[:, CW // 2 + KD * D + D:CW], w2b_s), (col[:], w3_s)]
        b1_s = sb("b1_s", [P, D], F32)
        b2_s = sb("b2_s", [P, D], F32)
        bh_s = sb("bh_s", [P, D], F32)
        b2a_s = sb("b2a_s", [P, P], F32)
        b2b_s = sb("b2b_s", [P, D], F32)
        b3_s = sb("b3_s", [P, D], F32)
        ident = sb("ident", [P, P], F32)
        ident_up = sb("ident_up", [P, P], F16)
        ones = sb("ones", [P, 1], F32)
        ln_eps = sb("ln_eps", [P, 1], F32)
        zero = sb("zero", [P, 1], F32)
        deg = sb("deg", [P, TILES], F32)
        none = sb("none", [P, GT], F32)
        sums = sb("sums", [P, 2, GT], F32)
        root = sb("root", [P, 2, GT], F32)
        root_scrap = sb("root_scrap", [P, 2, GT], F32)
        r_norm = sb("r_norm", [P, TILES], F32)
        r_last = sb("r_last", [P, TILES], F32)
        r_norm_down = sb("r_norm_down", [P, TILES], F32)
        r_last_down = sb("r_last_down", [P, TILES], F32)
        counts = r_last[:, 0:2 * CHUNKS].rearrange("p (i c) -> p i c", i=2)
        surplus = r_last_down[:, 0:CHUNKS]
        zero_rows = deg
        adj_r = sb("adj_r", [P, TILES], F32)
        stats = sb("stats", [P, GT, 6], F32)
        mv = sb("mv", [P, GT, 2], F32)
        std = sb("std", [P, GT], F32)
        guess = sb("guess", [P, GT], F32)
        scrap = sb("scrap", [P, GT], F32)
        rstd = sb("rstd", [P, GT], F32)
        shift = sb("shift", [P, GT], F32)

        main = [ps("main0", [P, GROUP]), ps("main1", [P, GROUP])]
        p_turn = ps("p_turn", [P, KD, GROUP])
        p_y = ps("p_y", [P, GT, D])
        p_h = ps("p_h", [P, GT, P])
        p_col = ps("p_col", [P, GROUP])

        masks = nc.dram_tensor("masks", (GROUPS, LOADS, P, PAIR, CW), U8, kind="Internal").ap()

        consts_set = sem("consts_set")
        ident_zero = sem("ident_zero")
        weights_in = sem("weights_in")
        bias_in = sem("bias_in")
        weights_hi_set = sem("weights_hi_set")
        weights_set = sem("weights_set")
        values_in = sem("values_in")
        mask_made = sem("mask_made")
        equal_counted = sem("equal_counted")
        surplus_found = sem("surplus_found")
        surplus_added = sem("surplus_added")
        mask_out = [sem(f"mask_out{i}") for i in range(RAW)]
        mask_in = [sem(f"mask_in{i}") for i in range(LOADS)]
        odd_step = sem("odd_step")
        odd_counted = sem("odd_counted")
        odd_summed = sem("odd_summed")
        one_value_set = sem("one_value_set")
        left = sem("left")

        class Signals:

            def __init__(self, way):
                self.raw_in = [sem(f"{way}_raw_in{s}") for s in range(RAW)]
                self.side_in = sem(f"{way}_side_in")
                self.x_again_in = sem(f"{way}_x_again_in")
                self.hi_cut = sem(f"{way}_hi_cut")
                self.lo_cut = sem(f"{way}_lo_cut")
                self.chunk_used = sem(f"{way}_chunk_used")
                self.half0_done = sem(f"{way}_half0_done")
                self.half_out = [sem(f"{way}_half0_out"), sem(f"{way}_half1_out")]
                self.fhi_set = sem(f"{way}_fhi_set")
                self.flo_set = sem(f"{way}_flo_set")
                self.y_done = sem(f"{way}_y_done")
                self.y_read = sem(f"{way}_y_read")
                self.v_set = sem(f"{way}_v_set")
                self.v_part = sem(f"{way}_v_part")
                self.relu_set = sem(f"{way}_relu_set")
                self.turned = sem(f"{way}_turned")
                self.side_hi_set = sem(f"{way}_side_hi_set")
                self.side_lo_set = sem(f"{way}_side_lo_set")
                self.agg_hi_set = [sem(f"{way}_agg_hi_set{h}") for h in range(2)]
                self.agg_lo_set = [sem(f"{way}_agg_lo_set{h}") for h in range(2)]
                self.pre_set = sem(f"{way}_pre_set")
                self.h_done = sem(f"{way}_h_done")
                self.stats_set = sem(f"{way}_stats_set")
                self.mv_set = sem(f"{way}_mv_set")
                self.std_set = sem(f"{way}_std_set")
                self.rstd_set = sem(f"{way}_rstd_set")
                self.shift_set = sem(f"{way}_shift_set")
                self.x_new = sem(f"{way}_x_new")
                self.x_kept = sem(f"{way}_x_kept")
                self.w_part = sem(f"{way}_w_part")
                self.w_set = sem(f"{way}_w_set")
                self.col_step = sem(f"{way}_col_step")
                self.col_set = sem(f"{way}_col_set")
                self.col_done = sem(f"{way}_col_done")
                self.deg_set = sem(f"{way}_deg_set")
                self.none_set = sem(f"{way}_none_set")
                self.root_in = sem(f"{way}_root_in")
                self.root_set = sem(f"{way}_root_set")
                self.recip_set = sem(f"{way}_recip_set")
                self.r_set = sem(f"{way}_r_set")
                self.adj_r_set = sem(f"{way}_adj_r_set")
                self.extra_set = sem(f"{way}_extra_set")
                self.out_set = sem(f"{way}_out_set")
                self.out_written = sem(f"{way}_out_written")
                self.own_turned = sem(f"{way}_own_turned")
                self.own_out = sem(f"{way}_own_out")
                self.agg_part = sem(f"{way}_agg_part")
                self.agg_set = [sem(f"{way}_agg_set{h}") for h in range(2)]
                self.guess_set = sem(f"{way}_guess_set")
                self.newton = sem(f"{way}_newton")
                self.root_newton = sem(f"{way}_root_newton")
                self.root_exact = sem(f"{way}_root_exact")

        x_piece_in = [sem(f"x_piece_in{c}") for c in range(CHUNKS)]
        by_mask = Signals("mask")
        by_parts = Signals("parts")

        def tail_of(l, g):
            if is_first(g):
                return l - 1, GROUPS - 1
            return l, g - 1

        def is_first(g):
            return isinstance(g, int) and g == 0

        def is_second(g):
            return isinstance(g, int) and g == 1

        def free(eng, semaphore, count):
            if not is_first(count):
                eng.wait_ge(semaphore, count)

        def steady(eng, *values):
            held = [v if isinstance(v, int) else eng.snap(eng.to_reg(v)) for v in values]
            eng.wait_ge(consts_set, 1)
            return held

        def half_of(t, tl, h):
            return t[:, 0, h * D:(h + 1) * D] if tl == NORM else t[:, h, :]

        def rows(t, g):
            return t[:, bass.ds(g * GT, GT)]

        def layer(eng, s, l, group):
            group(s, l, 0)
            group(s, l, 1)
            with eng.Fori(2, GROUPS) as g:
                group(s, l, g)

        def run(eng, group, last, decided, again):
            layer(eng, by_mask, CONV1, group)
            decided()
            eng.wait_ge(one_value_set, 1)
            flag = eng.value_load(one_value[0:1, 0:1], min_val=0, max_val=1)
            with eng.If(flag == 1):
                for l in range(CONV2, LAYERS):
                    layer(eng, by_mask, l, group)
                last(by_mask, LAST, GROUPS - 1)
            with eng.Else():
                eng.drain()
                eng.nop().then_inc(left, 1)
                eng.wait_ge(left, 5)
                again()
                for l in range(LAYERS):
                    layer(eng, by_parts, l, group)
                last(by_parts, LAST, GROUPS - 1)

        def nothing():
            pass

        def summed(s, l, g, c):
            if l == CONV2:
                return s.col_step, g * (CHUNKS + 1) + c + 1
            if l == HEADS:
                return s.col_step, GROUPS * (CHUNKS + 1) + g * TILES + (c + 1) * CT
            return s.chunk_used, 0

        block = ctx.enter_context(nc.Block())


        @block.gpsimd
        def _(pool):
            nc.gpsimd.memset(ident[:], 0.0)
            nc.gpsimd.memset(ident_up[:], 0.0).then_inc(ident_zero, 1)
            nc.gpsimd.memset(ones[:], 1.0)
            nc.gpsimd.memset(ln_eps[:], LN_EPS)
            nc.gpsimd.memset(zero[:], 0.0).then_inc(consts_set, 1)
            pool.wait_ge(ident_zero, 1)
            nc.gpsimd.affine_select(out=ident[:], in_=ident[:], compare_op=ALU.not_equal, fill=1.0,
                                    base=0, pattern=[[-1, P]], channel_multiplier=1).then_inc(consts_set, 1)
            nc.gpsimd.affine_select(out=ident_up[:], in_=ident_up[:], compare_op=ALU.not_equal, fill=A_UP,
                                    base=0, pattern=[[-1, P]], channel_multiplier=1).then_inc(consts_set, 1)

            pool.wait_ge(one_value_set, 1)
            flag = pool.value_load(one_value[0:1, 0:1], min_val=0, max_val=1)
            with pool.If(flag == 0):
                pool.drain()
                pool.nop().then_inc(left, 1)

        @block.sync
        def _(sp):
            def load_raw(s, l, g, c):
                k = (l * GROUPS + g) * CHUNKS + c
                if s is by_mask and not (is_first(g) and c < RAW):
                    sp.wait_ge(mask_made, k - RAW + 1)
                    sp.wait_ge(equal_counted, k - RAW + 1)
                if s is by_parts and not (l == 0 and is_first(g) and c < RAW):
                    read, count = summed(s, l, g, c - RAW) if c >= RAW else summed(s, *tail_of(l, g), c + CHUNKS - RAW)
                    done, count, g = steady(sp, k - RAW + 1, count, g)
                    sp.wait_ge(s.hi_cut, done)
                    sp.wait_ge(s.lo_cut, done)
                    free(sp, read, count)
                sp.dma_start(raw[:, c % RAW, :], adjT[g, c]).then_inc(s.raw_in[c % RAW], 16)

            def store_mask(g, c):
                made, g = steady(sp, g * CHUNKS + c + 1, g)
                sp.wait_ge(mask_made, made)
                sp.dma_start(masks[g, c // PAIR, :, c % PAIR, :], mask_made_ring[:, c % RAW, :].bitcast(U8)).then_inc(
                    mask_out[c % RAW], 16)

            def load_mask(s, l, g, q):
                tl, tg = tail_of(l, g)
                if tl >= CONV2:
                    read, count = summed(s, tl, tg, (q + 1) * PAIR - 1)
                    used, count, g = steady(sp, (tl * GROUPS + tg) * CHUNKS + (q + 1) * PAIR, count, g)
                    sp.wait_ge(s.chunk_used, used)
                    free(sp, read, count)
                sp.dma_start(mask_in_ring[:, q].bitcast(U8), masks[g, q]).then_inc(mask_in[q], 16)

            def load_side(s, g):
                free(sp, s.side_lo_set, g)
                sp.dma_start(w[:].rearrange("p a b -> p (a b)").rearrange("p (k n) -> p k n", k=KD),
                             xT_t[g]).then_inc(s.side_in, 16)

            def load_x_again(s, g):
                if is_first(g):
                    sp.wait_ge(s.side_lo_set, GROUPS)
                else:
                    sp.wait_ge(s.v_set, GROUPS + g)
                sp.dma_start(x_in[:], x_t[g]).then_inc(s.x_again_in, 16)

            def store(s, g):
                sp.wait_ge(s.out_set, g + 1)
                sp.dma_start(out_t[g], u[:]).then_inc(s.out_written, 16)

            def tail(s, tl, tg, c):
                if tl == CONV1 and c == 0:
                    load_side(s, tg)
                if tl == CONV2 and c == 0:
                    load_x_again(s, tg)
                if tl == LAST and c == CHUNKS - 1:
                    store(s, tg)

            def group(s, l, g):
                first = l == CONV1 and is_first(g)
                for c in range(CHUNKS):
                    if first:
                        sp.dma_start(xs[:, c * GT:(c + 1) * GT, :], x_t[c]).then_inc(x_piece_in[c], 16)
                    if s is by_mask and l == CONV1 and c == (1 if is_first(g) else 0):
                        at = bass.ds(g * GROUP, GROUP)
                        sp.dma_start(value_cols[:, at], diag[at].partition_broadcast(P)).then_inc(values_in, 16)
                    if s is by_mask and l == CONV1:
                        if c >= 3:
                            store_mask(g, c - 3)
                        elif not is_first(g):
                            store_mask(g - 1, c + CHUNKS - 3)
                    if s is by_parts or l == CONV1:
                        load_raw(s, l, g, c)
                    elif c % PAIR == 0 and not (l == CONV2 and is_first(g)):
                        load_mask(s, l, g, c // PAIR)
                    if s is by_mask and l == CONV1 and (first and c == CHUNKS - 1 or is_second(g) and c == 6):
                        some = slice(0, 1) if first else slice(1, None)
                        for (stage, cut_into), src in list(zip(staged, (w1, w2, wh, w2a, w2b, w3)))[some]:
                            k, n = cut_into.shape[2:]
                            sp.dma_start(stage.rearrange("p (k n) -> p k n", k=k),
                                         src.rearrange("(k p) n -> p k n", p=P)).then_inc(weights_in, 16)
                    if s is by_mask and l == CONV1 and is_second(g) and c == 1:
                        sp.dma_start(b1_s[:], b1.partition_broadcast(P)).then_inc(bias_in, 16)
                    if s is by_mask and l == CONV1 and is_second(g) and c == 6:
                        sp.dma_start(value_rows[:], diagT).then_inc(weights_in, 16)
                        for dst, src in ((b2_s, b2), (bh_s, bh), (b2a_s, b2a), (b2b_s, b2b), (b3_s, b3)):
                            sp.dma_start(dst[:], src.partition_broadcast(P)).then_inc(weights_in, 16)
                    tail(s, *tail_of(l, g), c)

            def last(s, tl, tg):
                for c in range(CHUNKS):
                    tail(s, tl, tg, c)
                sp.wait_ge(s.out_written, 16 * GROUPS)

            def decided():
                for c in range(CHUNKS - 3, CHUNKS):
                    store_mask(GROUPS - 1, c)
                sp.wait_ge(equal_counted, GROUPS * CHUNKS)
                for i in range(RAW):
                    sp.wait_ge(mask_out[i], 16 * (CHUNKS // RAW))
                for q in range(LOADS):
                    load_mask(by_mask, CONV2, 0, q)
                for i in range(RAW):
                    sp.wait_ge(mask_out[i], 16 * GROUPS * (CHUNKS // RAW))

            def again():
                for q in range(LOADS):
                    sp.wait_ge(mask_in[q], 16)

            run(sp, group, last, decided, again)

        def cut_at(c):
            return staged[0:1] if c == 0 else staged[1:] if c == 7 else []

        WEIGHTS = 16 * 12

        @block.tensor
        def _(pe):
            def products(s, l, g, c, ready, count, terms):
                buf = l % 2
                count, emptied = steady(pe, count, l * GROUPS + g)
                ready(count)
                pe.wait_ge(s.fhi_set, l * GROUPS + c + 1)
                pe.wait_ge(s.flo_set, l * GROUPS + c + 1)
                for h in range(2):
                    if c == 0 and not (l == CONV1 and is_first(g)):
                        if h == 1:
                            steady(pe)
                        pe.wait_ge(s.half_out[h], emptied)
                    for t in range(CT):
                        m = c * CT + t
                        if l == NORM:
                            at = slice(t * GROUP + h * D, t * GROUP + (h + 1) * D)
                            feat, o = slice(0, P), main[h][:, 0:D]
                        else:
                            at = slice(t * GROUP, (t + 1) * GROUP)
                            feat, o = slice(h * P, (h + 1) * P), main[h][:]
                        for i, (features, chunk) in enumerate(terms):
                            last = nc.tensor.matmul(o, features[:, buf, m, feat], chunk[:, at],
                                                    start=(m == 0 and i == 0),
                                                    stop=(m == TILES - 1 and i == len(terms) - 1
                                                          and not (l == NORM and s is by_parts)))
                    if c == CHUNKS - 1 and l == NORM and s is by_parts:
                        for j in (2 * h, 2 * h + 1):
                            o = main[h][:, (j % 2) * P:(j % 2 + 1) * P]
                            last = own_features(g, j, o, start=False, stop=(j % 2 == 1))
                    if c == CHUNKS - 1 and h == 0:
                        last.then_inc(s.half0_done, 1)
                last.then_inc(s.chunk_used, 1)

            def own_features(g, j, o, start, stop):
                for n, part in enumerate((f_hi, f_lo)):
                    own = part[:, NORM % 2, bass.ds(g * GT + j, 1), 0:P].rearrange("p a b -> p (a b)")
                    last = nc.tensor.matmul(o, own, ident_up[:], start=start and n == 0, stop=stop and n == 1)
                return last

            def stream(s, l, g, c):
                k = (l * GROUPS + g) * CHUNKS + c

                def parts_ready(count):
                    pe.wait_ge(s.hi_cut, count)
                    pe.wait_ge(s.lo_cut, count)

                def made_ready(count):
                    pe.wait_ge(mask_made, count)

                def mask_ready(count):
                    pe.wait_ge(mask_in[c // PAIR], count)

                if s is by_parts:
                    upper, lower = a_hi[:, c % CUT, :], a_lo[:, c % CUT, :]
                    products(s, l, g, c, parts_ready, k + 1, [(f_hi, upper), (f_hi, lower), (f_lo, upper)])
                elif l == CONV1:
                    mask = mask_made_ring[:, c % RAW, :]
                    products(s, l, g, c, made_ready, k + 1, [(f_hi, mask), (f_lo, mask)])
                else:
                    mask = mask_in_ring[:, c // PAIR, c % PAIR, :]
                    products(s, l, g, c, mask_ready, 16 * ((l - CONV2) * GROUPS + g + 1), [(f_hi, mask), (f_lo, mask)])

            def turn_own(s, tg):
                pe.wait_ge(s.side_lo_set, 3 * GROUPS)
                free(pe, s.own_out, tg)
                for j in range(GT):
                    last = own_features(tg, j, p_turn[:, 0, j * P:(j + 1) * P], start=True, stop=True)
                last.then_inc(s.own_turned, 1)

            def turn_hidden(s, tg):
                if is_first(tg):
                    pe.wait_ge(consts_set, 3)
                pe.wait_ge(s.side_lo_set, GROUPS + tg)
                for h in range(KD):
                    for j in range(GT):
                        for part in (f_hi, f_lo):
                            own = part[:, 1, bass.ds(tg * GT + j, 1), h * P:(h + 1) * P].rearrange("p a b -> p (a b)")
                            last = nc.tensor.matmul(p_turn[:, h, j * P:(j + 1) * P], own, ident_up[:],
                                                    start=part is f_hi, stop=part is f_lo)
                last.then_inc(s.turned, 1)

            def turn_new(s, tg):
                pe.wait_ge(s.x_new, GROUPS + tg + 1)
                pe.wait_ge(s.side_lo_set, 2 * GROUPS + tg)
                for h in range(KD):
                    for j in range(GT):
                        last = nc.tensor.transpose(p_turn[:, h, j * P:(j + 1) * P], u[:, j, h * P:(h + 1) * P], ident[:])
                last.then_inc(s.turned, 1)

            def times(o, rows_hi, rows_lo, weights, start, stop):
                nc.tensor.matmul(o, rows_hi, weights[0], start=start, stop=False)
                nc.tensor.matmul(o, rows_hi, weights[1], start=False, stop=False)
                return nc.tensor.matmul(o, rows_lo, weights[0], start=False, stop=stop)

            def product(s, tl, tg):
                n = tl * GROUPS + tg
                free(pe, s.v_set, n)
                if tl == CONV1 and is_first(tg):
                    pe.wait_ge(weights_set, 1)
                if tl == CONV2 and is_first(tg):
                    pe.wait_ge(weights_set, len(staged))
                weights = {CONV1: w1_s, CONV2: w2_s, HEADS: wh_s, NORM: w2b_s, LAST: w3_s}[tl]
                own = KD if tl in (CONV1, CONV2) else 0
                if own:
                    pe.wait_ge(s.side_lo_set, n + 1)
                for k in range(own):
                    for j in range(GT):
                        at = slice(j * P, (j + 1) * P)
                        times(p_y[:, j, :], side_hi[:, k, at], side_lo[:, k, at], (weights[:, 0, k], weights[:, 1, k]),
                              start=(k == 0 and j % 2 == 0), stop=False)
                for h in range(2):
                    if h == 1:
                        steady(pe)
                    pe.wait_ge(s.agg_lo_set[h], n + 1)
                    k = 0 if tl == NORM else h
                    for j in range(2 * h, 2 * h + 2) if tl == NORM else range(GT):
                        at = slice(j * P, (j + 1) * P)
                        last = times(p_y[:, j, :], agg_hi[:, k, at], agg_lo[:, k, at],
                                     (weights[:, 0, own + k], weights[:, 1, own + k]),
                                     start=(own + h == 0 and j % 2 == 0) or tl == NORM, stop=(h == 1 and j % 2 == 1) or tl == NORM)
                last.then_inc(s.y_done, 1)

            def hidden(s, tg):
                pe.wait_ge(s.side_lo_set, 2 * GROUPS + tg + 1)
                free(pe, s.w_part, tg)
                for j in range(GT):
                    at = slice(j * P, (j + 1) * P)
                    for k in range(KD):
                        last = times(p_h[:, j, :], side_hi[:, k, at], side_lo[:, k, at], (w2a_s[:, 0, k], w2a_s[:, 1, k]),
                                     start=(k == 0), stop=(k == KD - 1))
                last.then_inc(s.h_done, 1)

            def columns(s, tl, tg):
                n = (tl - CONV2) * GROUPS + tg
                pe.wait_ge(s.col_set, n + 1)
                if is_first(n):
                    pe.wait_ge(consts_set, 1)
                free(pe, s.deg_set, tg if tl == CONV2 else GROUPS)
                if tl == HEADS:
                    free(pe, s.adj_r_set, tg)
                for j in range(GT):
                    last = nc.tensor.matmul(p_col[:, j:j + 1], col[:, j * P:(j + 1) * P], ones[:], start=True, stop=True)
                last.then_inc(s.col_done, 1)

            def tail(s, tl, tg, c):
                if tl == CONV2 and c == 0:
                    turn_hidden(s, tg)
                if tl >= 0 and c == (1 if tl == HEADS else 2):
                    product(s, tl, tg)
                if tl in (CONV2, HEADS) and c == 1:
                    columns(s, tl, tg)
                if tl == HEADS and c == 4:
                    turn_new(s, tg)
                if tl == HEADS and c == 5:
                    hidden(s, tg)

            def group(s, l, g):
                for c in range(CHUNKS):
                    stream(s, l, g, c)
                    if l == NORM and s is by_mask and c == 6:
                        turn_own(s, g)
                    tail(s, *tail_of(l, g), c)

            def last(s, tl, tg):
                for c in range(CHUNKS):
                    tail(s, tl, tg, c)

            def decided():
                pe.wait_ge(odd_counted, 1)
                nc.tensor.matmul(p_h[0:1, 0, 0:2], ones[:], odd_ones[:], start=True, stop=True).then_inc(odd_summed, 1)

            run(pe, group, last, decided, nothing)

        @block.scalar
        def _(act):
            def first_features(s, c):
                act.wait_ge(x_piece_in[c], 16 if s is by_mask else 32)
                nc.scalar.activation(f_hi[:, 0, c * GT:(c + 1) * GT, :], xs[:, c * GT:(c + 1) * GT, :], ACT.Copy,
                                     scale=F_UP).then_inc(s.fhi_set, 1)

            def stream(s, l, g, c):
                k = (l * GROUPS + g) * CHUNKS + c
                came = 16 * ((l * GROUPS + g) * (CHUNKS // RAW) + c // RAW + 1)
                if s is by_parts:
                    act.wait_ge(s.raw_in[c % RAW], came)
                    if not (l == 0 and is_first(g) and c < CUT):
                        act.wait_ge(s.chunk_used, k - CUT + 1)
                    nc.scalar.activation(a_hi[:, c % CUT, :], raw[:, c % RAW, :], ACT.Copy, scale=A_UP).then_inc(s.hi_cut, 1)
                elif l == CONV1:
                    came, used, written, read = steady(act, came, k - RAW + 1, 16 * (g * (CHUNKS // RAW) + c // RAW), g)
                    act.wait_ge(s.raw_in[c % RAW], came)
                    if not (is_first(g) and c < RAW):
                        act.wait_ge(s.chunk_used, used)
                        act.wait_ge(mask_out[c % RAW], written)
                    if c == 0:
                        free(act, surplus_added, read)
                    nc.scalar.activation(mask_made_ring[:, c % RAW, :], raw[:, c % RAW, :].bitcast(U32), ACT.Sign,
                                         saturate=False, accum_out=counts[:, 0, c:c + 1]).then_inc(mask_made, 1)

            def cut_weights(c):
                if c == 0:
                    act.wait_ge(weights_in, 16)
                if c == 7:
                    act.wait_ge(weights_in, WEIGHTS)
                for stage, cut_into in cut_at(c):
                    nc.scalar.activation(cut_into[:, 0].rearrange("p k n -> p (k n)"), stage, ACT.Copy,
                                         scale=W_UP).then_inc(weights_hi_set, 1)

            def tail(s, tl, tg, c):
                if tl < 0:
                    return
                n = tl * GROUPS + tg
                wide = D if tl == NORM else GROUP
                if c == 0:
                    act.wait_ge(s.half0_done, n + 1)
                    free(act, s.agg_lo_set[0], n)
                    nc.scalar.activation(half_of(agg, tl, 0), main[0][:, 0:wide], ACT.Copy,
                                         scale=1.0 if s is by_mask else 1.0 / A_UP).then_inc(s.half_out[0], 1)
                    if s is by_mask:
                        act.wait_ge(s.chunk_used, CHUNKS * (n + 1))
                        free(act, s.agg_lo_set[1], n)
                        nc.scalar.activation(half_of(agg, tl, 1), main[1][:, 0:wide], ACT.Copy).then_inc(s.half_out[1], 1)
                    if tl == NORM and s is by_mask:
                        act.wait_ge(s.own_turned, tg + 1)
                        act.wait_ge(s.h_done, GROUPS)
                        act.wait_ge(s.agg_set[1], n)
                        nc.scalar.activation(side[:, 0, :], p_turn[:, 0, :], ACT.Copy, scale=1.0 / A_UP).then_inc(s.own_out, 1)
                if c == 1:
                    if tl == CONV1:
                        act.wait_ge(s.side_in, 16 * (tg + 1))
                        free(act, s.y_done, n)
                        nc.scalar.activation(side_hi.rearrange("p k n -> p (k n)"), w[:].rearrange("p a b -> p (a b)"),
                                             ACT.Copy, scale=F_UP).then_inc(s.side_hi_set, 1)
                    if tl == CONV2:
                        act.wait_ge(s.turned, tg + 1)
                        act.wait_ge(s.y_done, n)
                        nc.scalar.activation(side_hi, p_turn[:], ACT.Copy, scale=1.0 / A_UP).then_inc(s.side_hi_set, 1)
                    free(act, s.y_done, n)
                    ready = s.agg_set if s is by_mask else s.half_out
                    for h in range(2):
                        act.wait_ge(ready[h], n + 1)
                        nc.scalar.activation(half_of(agg_hi, tl, h), half_of(agg, tl, h), ACT.Copy).then_inc(s.agg_hi_set[h], 1)
                if tl == CONV1 and c == 5:
                    act.wait_ge(s.v_set, n + 1)
                    nc.scalar.activation(rows(xs, tg), v[:], ACT.Relu).then_inc(s.relu_set, 1)
                    nc.scalar.activation(f_hi[:, 1, bass.ds(tg * GT, GT), :], v[:], ACT.Relu, scale=F_UP).then_inc(s.fhi_set, 1)
                if tl == CONV2 and c == 2:
                    act.wait_ge(s.root_in, tg + 1)
                    nc.scalar.activation(root[:], sums[:], ACT.Sqrt, bias=zero[:]).then_inc(s.root_set, 1)
                if tl >= CONV2 and c == (2 if tl == HEADS else 3):
                    act.wait_ge(s.mv_set, (tl - CONV2) * GROUPS + tg + 1)
                    nc.scalar.activation(std[:], mv[:, :, 1:2].rearrange("p a b -> p (a b)"), ACT.Sqrt,
                                         bias=ln_eps[:]).then_inc(s.std_set, 1)
                if tl == HEADS and c == 2:
                    act.wait_ge(s.shift_set, tg + 1)
                    free(act, s.turned, GROUPS + tg)
                    for j in range(GT):
                        last = nc.scalar.activation(u[:, j, :], v[:, j, :], ACT.Identity, scale=rstd[:, j:j + 1],
                                                    bias=shift[:, j:j + 1])
                    last.then_inc(s.x_new, 1)
                if tl == CONV2 and c == 4:
                    act.wait_ge(s.x_new, tg + 1)
                    nc.scalar.activation(f_hi[:, 0, bass.ds(tg * GT, GT), :], rows(xs, tg), ACT.Copy,
                                         scale=F_UP).then_inc(s.fhi_set, 1)
                if tl == HEADS and c == 4:
                    act.wait_ge(s.x_new, GROUPS + tg + 1)
                    nc.scalar.activation(rows(xs, tg), u[:], ACT.Copy).then_inc(s.x_kept, 1)
                if tl == HEADS and c == 4:
                    act.wait_ge(s.turned, GROUPS + tg + 1)
                    act.wait_ge(s.y_done, 2 * GROUPS)
                    free(act, s.h_done, tg)
                    nc.scalar.activation(side_hi, p_turn[:], ACT.Copy, scale=F_UP).then_inc(s.side_hi_set, 1)
                if tl in (HEADS, NORM) and c == (6 if tl == HEADS else 4):
                    act.wait_ge(s.w_set, (tl - HEADS) * GROUPS + tg + 1)
                    wide = P if tl == HEADS else D
                    nc.scalar.activation(f_hi[:, (tl + 1) % 2, bass.ds(tg * GT, GT), 0:wide], w[:, :, 0:wide], ACT.Copy,
                                         scale=F_UP).then_inc(s.fhi_set, 1)

            def group(s, l, g):
                if l == CONV1 and is_first(g):
                    act.wait_ge(consts_set, 1)
                for c in range(CHUNKS):
                    if l == CONV1 and is_first(g):
                        first_features(s, c)
                    stream(s, l, g, c)
                    tail(s, *tail_of(l, g), c)
                    if s is by_mask and l == CONV1 and is_second(g):
                        cut_weights(c)

            def last(s, tl, tg):
                for c in range(CHUNKS):
                    tail(s, tl, tg, c)

            run(act, group, last, nothing, nothing)

        @block.vector
        def _(dve):
            def cut_low(dst, src, upper, up):
                return nc.vector.scalar_tensor_tensor(out=dst, in0=src, scalar=up, in1=upper,
                                                      op0=ALU.mult, op1=ALU.subtract)

            def first_features(s, c):
                at = slice(c * GT, (c + 1) * GT)
                dve.wait_ge(x_piece_in[c], 16 if s is by_mask else 32)
                dve.wait_ge(s.fhi_set, c + 1)
                cut_low(f_lo[:, 0, at, :].rearrange("p a b -> p (a b)"), xs[:, at, :].rearrange("p a b -> p (a b)"),
                        f_hi[:, 0, at, :].rearrange("p a b -> p (a b)"), F_UP).then_inc(s.flo_set, 1)

            def stream(s, l, g, c):
                k = (l * GROUPS + g) * CHUNKS + c
                came = 0
                if s is by_parts:
                    chunk = raw[:, c % RAW, :]
                    dve.wait_ge(s.raw_in[c % RAW], 16 * ((l * GROUPS + g) * (CHUNKS // RAW) + c // RAW + 1))
                    dve.wait_ge(s.hi_cut, k + 1)
                    if not (l == 0 and is_first(g) and c < CUT):
                        dve.wait_ge(s.chunk_used, k - CUT + 1)
                    cut_low(a_lo[:, c % CUT, :], chunk, a_hi[:, c % CUT, :], A_UP).then_inc(s.lo_cut, 1)
                elif l == CONV1:
                    chunk = raw[:, c % RAW, :].rearrange("p (t n) -> p t n", t=CT)
                    values = value_cols[:, bass.ds(g * GROUP, GROUP)].unsqueeze(1).to_broadcast([P, CT, GROUP])
                    scrap = colw[:, 0:CW // 2].bitcast(BF16).rearrange("p (t n) -> p t n", t=CT)
                    dve.wait_ge(s.raw_in[c % RAW], 16 * (g * (CHUNKS // RAW) + c // RAW + 1))
                    free(dve, equal_counted, k)
                    if c == 0:
                        free(dve, surplus_added, g)
                    nc.vector.scalar_tensor_tensor(out=scrap, in0=chunk, scalar=1.0, in1=values, op0=ALU.mult,
                                                   op1=ALU.is_equal,
                                                   accum_out=counts[:, 1, c:c + 1],
                                                   ).then_inc(equal_counted, 1)
                    if c == CHUNKS - 1:
                        dve.wait_ge(equal_counted, k + 1)
                        dve.wait_ge(mask_made, k + 1)
                        if is_first(g):
                            nc.vector.tensor_tensor(surplus[:], counts[:, 0, :], counts[:, 1, :], ALU.subtract).then_inc(surplus_added, 1)
                        else:
                            nc.vector.tensor_tensor(counts[:, 0, :], counts[:, 0, :], counts[:, 1, :], ALU.subtract).then_inc(surplus_found, 1)
                            dve.wait_ge(surplus_found, g)
                            nc.vector.tensor_tensor(surplus[:], surplus[:], counts[:, 0, :], ALU.add).then_inc(surplus_added, 1)
                else:
                    chunk = mask_in_ring[:, c // PAIR, c % PAIR, :]
                    came = 16 * ((l - CONV2) * GROUPS + g + 1)
                if l == CONV2:
                    n = g * (CHUNKS + 1)
                    if c == 0:
                        came, read = steady(dve, came, g) if s is by_mask else (came, g)
                        if s is by_mask:
                            dve.wait_ge(mask_in[c // PAIR], came)
                        free(dve, s.col_set, read)
                        nc.vector.tensor_copy(colw[:], chunk).then_inc(s.col_step, 1)
                    else:
                        came, before = steady(dve, came, n + c) if s is by_mask else (came, n + c)
                        if s is by_mask:
                            dve.wait_ge(mask_in[c // PAIR], came)
                        dve.wait_ge(s.col_step, before)
                        nc.vector.tensor_tensor(colw[:], colw[:], chunk, ALU.add).then_inc(s.col_step, 1)
                    if c == CHUNKS - 1:
                        dve.wait_ge(s.col_step, n + CHUNKS)
                        nc.vector.tensor_tensor(colw[:, 0:2 * GROUP], colw[:, 0:2 * GROUP], colw[:, 2 * GROUP:],
                                                ALU.add).then_inc(s.col_step, 1)
                        dve.wait_ge(s.col_step, n + CHUNKS + 1)
                        free(dve, s.col_done, g)
                        nc.vector.tensor_tensor(col[:], colw[:, 0:GROUP], colw[:, GROUP:2 * GROUP],
                                                ALU.add).then_inc(s.col_set, 1)
                if l == HEADS:
                    n = GROUPS * (CHUNKS + 1) + g * TILES
                    dve.wait_ge(s.r_set, c + 1 if is_first(g) else GROUPS)
                    for t in range(CT):
                        m = c * CT + t
                        part = chunk[:, t * GROUP:(t + 1) * GROUP]
                        r = r_norm[:, m:m + 1]
                        under_way = colw[:, (m % 2) * GROUP:(m % 2 + 1) * GROUP]
                        came, before, read = steady(dve, came, n + m - 1, GROUPS + g) if s is by_mask else (came, n + m - 1, GROUPS + g)
                        if s is by_mask and t == 0:
                            dve.wait_ge(mask_in[c // PAIR], came)
                        if m == 0:
                            dve.wait_ge(s.col_set, read)
                        if m < 2:
                            nc.vector.tensor_scalar(under_way, part, r, None, ALU.mult).then_inc(s.col_step, 1)
                        else:
                            dve.wait_ge(s.col_step, before)
                            nc.vector.scalar_tensor_tensor(out=under_way, in0=part, scalar=r, in1=under_way,
                                                           op0=ALU.mult, op1=ALU.add).then_inc(s.col_step, 1)
                    if c == CHUNKS - 1:
                        dve.wait_ge(s.col_step, n + TILES)
                        dve.wait_ge(s.col_done, GROUPS + g)
                        nc.vector.tensor_tensor(col[:], colw[:, 0:GROUP], colw[:, GROUP:2 * GROUP], ALU.add).then_inc(s.col_set, 1)

            def bias(t):
                return t[:].unsqueeze(1).to_broadcast([P, GT, t.shape[1]])

            def inverse_root(dst, value, eps, guess, scrap, step, n, done):
                nc.vector.scalar_tensor_tensor(out=scrap, in0=value, scalar=eps, in1=guess, op0=ALU.add,
                                               op1=ALU.mult).then_inc(step, 1)
                dve.wait_ge(step, 2 * n + 1)
                nc.vector.scalar_tensor_tensor(out=scrap, in0=scrap, scalar=-0.5, in1=guess, op0=ALU.mult,
                                               op1=ALU.mult).then_inc(step, 1)
                dve.wait_ge(step, 2 * n + 2)
                nc.vector.scalar_tensor_tensor(out=dst, in0=scrap, scalar=1.5, in1=guess, op0=ALU.add,
                                               op1=ALU.mult).then_inc(done, 1)

            def norm(s, tl, tg, dst=None):
                n = (tl - CONV2) * GROUPS + tg
                dve.wait_ge(s.v_set, tl * GROUPS + tg + 1)
                for j in range(GT):
                    last = nc.vector.bn_stats(stats[:, j, :], v[:, j, :])
                last.then_inc(s.stats_set, 1)
                now, = steady(dve, n + 1)
                dve.wait_ge(s.stats_set, now)
                for j in range(GT):
                    last = nc.vector.bn_aggr(mv[:, j, :], stats[:, j, :])
                last.then_inc(s.mv_set, 1)
                dve.wait_ge(s.std_set, n + 1)
                nc.vector.reciprocal(guess[:], std[:]).then_inc(s.guess_set, 1)
                dve.wait_ge(s.guess_set, n + 1)
                inverse_root(rstd[:].unsqueeze(2), mv[:, :, 1:2], LN_EPS, guess[:].unsqueeze(2), scrap[:].unsqueeze(2),
                             s.newton, n, s.rstd_set)
                dve.wait_ge(s.rstd_set, n + 1)
                if dst is None:
                    return nc.vector.scalar_tensor_tensor(out=shift[:].unsqueeze(2), in0=mv[:, :, 0:1], scalar=-1.0,
                                                          in1=rstd[:].unsqueeze(2), op0=ALU.mult, op1=ALU.mult)
                for j in range(GT):
                    last = nc.vector.tensor_scalar(dst(j), v[:, j, :], mv[:, j, 0:1], rstd[:, j:j + 1],
                                                   ALU.subtract, ALU.mult)
                return last

            def cut_w(s, tl, tg):
                wide = P if tl == HEADS else D
                dve.wait_ge(s.fhi_set, (tl + 1) * GROUPS + tg + 1)
                nc.vector.scalar_tensor_tensor(out=f_lo[:, (tl + 1) % 2, bass.ds(tg * GT, GT), 0:wide],
                                               in0=w[:, :, 0:wide], scalar=F_UP,
                                               in1=f_hi[:, (tl + 1) % 2, bass.ds(tg * GT, GT), 0:wide],
                                               op0=ALU.mult, op1=ALU.subtract).then_inc(s.flo_set, 1)

            def cut_weights(c):
                for i, (stage, cut_into) in enumerate(cut_at(c)):
                    dve.wait_ge(weights_hi_set, i + 1 if c == 0 else i + 2)
                    cut_low(cut_into[:, 1].rearrange("p k n -> p (k n)"), stage,
                            cut_into[:, 0].rearrange("p k n -> p (k n)"), W_UP).then_inc(weights_set, 1)

            def v_from_y(first):
                return nc.vector.scalar_tensor_tensor(out=v[:], in0=p_y[:], scalar=DOWN, in1=first, op0=ALU.mult, op1=ALU.add)

            def v_from_scaled_y(scale, tg):
                for j in range(GT):
                    last = nc.vector.scalar_tensor_tensor(out=v[:, j, :], in0=p_y[:, j, :], scalar=scale[:, bass.ds(tg * GT + j, 1)],
                                                          in1=v[:, j, :], op0=ALU.mult, op1=ALU.add)
                return last

            def tail(s, tl, tg, c):
                if tl < 0:
                    return
                n = tl * GROUPS + tg
                at = bass.ds(tg * GT, GT)
                if c == 0 and s is by_parts:
                    dve.wait_ge(s.chunk_used, CHUNKS * (n + 1))
                    free(dve, s.agg_lo_set[1], n)
                    wide = D if tl == NORM else GROUP
                    nc.vector.tensor_scalar(half_of(agg, tl, 1), main[1][:, 0:wide], 1.0 / A_UP, None, ALU.mult).then_inc(s.half_out[1], 1)
                if c == 0 and s is by_mask:
                    for h in range(2):
                        part = half_of(agg, tl, h)
                        dve.wait_ge(s.half_out[h], n + 1)
                        if tl == NORM:
                            value = value_cols[:, bass.ds(tg * GROUP + h * D, D)]
                            nc.vector.tensor_tensor(part, part, value, ALU.mult).then_inc(s.agg_part, 1)
                            dve.wait_ge(s.agg_part, 2 * tg + h + 1)
                            dve.wait_ge(s.own_out, tg + 1)
                            nc.vector.tensor_tensor(part, part, half_of(side, tl, h), ALU.add).then_inc(s.agg_set[h], 1)
                        else:
                            value = value_cols[:, bass.ds(tg * GROUP, GROUP)]
                            nc.vector.tensor_tensor(part, part, value, ALU.mult).then_inc(s.agg_set[h], 1)
                if c == 1:
                    if tl == CONV1:
                        dve.wait_ge(s.side_hi_set, n + 1)
                        cut_low(side_lo.rearrange("p k n -> p (k n)"), w[:].rearrange("p a b -> p (a b)"),
                                side_hi.rearrange("p k n -> p (k n)"), F_UP).then_inc(s.side_lo_set, 1)
                    if tl == CONV2:
                        dve.wait_ge(s.side_hi_set, n + 1)
                        cut_low(side_lo, p_turn[:], side_hi, 1.0 / A_UP).then_inc(s.side_lo_set, 1)
                    for h in range(2):
                        dve.wait_ge(s.agg_hi_set[h], n + 1)
                        nc.vector.tensor_tensor(half_of(agg_lo, tl, h), half_of(agg, tl, h), half_of(agg_hi, tl, h),
                                                ALU.subtract).then_inc(s.agg_lo_set[h], 1)
                if tl == CONV2 and c == 2:
                    dve.wait_ge(s.col_done, tg + 1)
                    if s is by_mask:
                        nc.vector.tensor_tensor(rows(deg, tg), p_col[:, 0:GT], rows(value_rows, tg), ALU.mult).then_inc(s.deg_set, 1)
                    else:
                        nc.vector.tensor_copy(rows(deg, tg), p_col[:, 0:GT]).then_inc(s.deg_set, 1)
                    dve.wait_ge(s.deg_set, tg + 1)
                    free(dve, s.r_set, tg)
                    nc.vector.tensor_scalar(none[:], rows(deg, tg), 1.0, 0.0, ALU.add, ALU.is_equal).then_inc(s.none_set, 1)
                    nc.vector.tensor_scalar(sums[:, 1, :], rows(deg, tg), DEG_EPS, None, ALU.add)
                    dve.wait_ge(s.none_set, 2 * tg + 1)
                    nc.vector.scalar_tensor_tensor(out=sums[:, 0, :], in0=rows(deg, tg), scalar=1.0, in1=none[:],
                                                   op0=ALU.add, op1=ALU.add).then_inc(s.root_in, 1)
                if tl == CONV2 and c == 2:
                    dve.wait_ge(s.root_set, tg + 1)
                    nc.vector.reciprocal(root[:], root[:]).then_inc(s.recip_set, 1)
                    nc.vector.tensor_scalar(none[:], none[:], -1.0, 1.0, ALU.mult, ALU.add).then_inc(s.none_set, 1)
                    dve.wait_ge(s.recip_set, tg + 1)
                    inverse_root(root[:], sums[:], 0.0, root[:], root_scrap[:], s.root_newton, tg, s.root_exact)
                    dve.wait_ge(s.none_set, 2 * tg + 2)
                    dve.wait_ge(s.root_exact, tg + 1)
                    nc.vector.tensor_copy(rows(r_last, tg), root[:, 1, :])
                    nc.vector.tensor_scalar(rows(r_last_down, tg), root[:, 1, :], DOWN, None, ALU.mult)
                    nc.vector.scalar_tensor_tensor(out=rows(r_norm_down, tg), in0=root[:, 0, :], scalar=DOWN, in1=none[:],
                                                   op0=ALU.mult, op1=ALU.mult)
                    nc.vector.tensor_tensor(rows(r_norm, tg), root[:, 0, :], none[:], ALU.mult).then_inc(s.r_set, 1)
                if tl == HEADS and c == 2:
                    dve.wait_ge(s.col_done, GROUPS + tg + 1)
                    if s is by_mask:
                        nc.vector.tensor_tensor(rows(adj_r, tg), p_col[:, 0:GT], rows(value_rows, tg), ALU.mult).then_inc(s.adj_r_set, 1)
                    else:
                        nc.vector.tensor_copy(rows(adj_r, tg), p_col[:, 0:GT]).then_inc(s.adj_r_set, 1)
                if tl == CONV1 and c == 5:
                    dve.wait_ge(s.y_done, n + 1)
                    if is_first(tg):
                        dve.wait_ge(bias_in, 16)
                    free(dve, s.fhi_set, GROUPS + tg)
                    free(dve, s.relu_set, tg)
                    v_from_y(bias(b1_s)).then_inc(s.v_set, 1)
                    dve.wait_ge(s.relu_set, tg + 1)
                    dve.wait_ge(s.fhi_set, GROUPS + tg + 1)
                    cut_low(f_lo[:, 1, at, :], xs[:, at, :], f_hi[:, 1, at, :], F_UP).then_inc(s.flo_set, 1)
                if tl == CONV2 and c == 3:
                    dve.wait_ge(s.y_done, n + 1)
                    v_from_y(bias(b2_s)).then_inc(s.y_read, 1)
                    dve.wait_ge(s.y_read, tg + 1)
                    nc.vector.scalar_tensor_tensor(out=v[:], in0=v[:], scalar=0.0, in1=rows(xs, tg), op0=ALU.max,
                                                   op1=ALU.add).then_inc(s.v_part, 1)
                    dve.wait_ge(s.v_part, tg + 1)
                    dve.wait_ge(s.x_again_in, 16 * (tg + 1))
                    nc.vector.scalar_tensor_tensor(out=v[:], in0=v[:], scalar=0.0, in1=x_in[:], op0=ALU.max,
                                                   op1=ALU.add).then_inc(s.v_set, 1)
                    norm(s, tl, tg, lambda j: xs[:, bass.ds(tg * GT + j, 1), :].rearrange("p a b -> p (a b)")).then_inc(s.x_new, 1)
                if tl == CONV2 and c == 4:
                    dve.wait_ge(s.fhi_set, 2 * GROUPS + tg + 1)
                    cut_low(f_lo[:, 0, at, :], xs[:, at, :], f_hi[:, 0, at, :], F_UP).then_inc(s.flo_set, 1)
                if tl == HEADS and c == 1:
                    dve.wait_ge(s.x_new, GROUPS + tg)
                    nc.vector.tensor_tensor(v[:], rows(xs, tg), bias(bh_s), ALU.add).then_inc(s.pre_set, 1)
                if tl == HEADS and c == 2:
                    dve.wait_ge(s.y_done, n + 1)
                    dve.wait_ge(s.pre_set, tg + 1)
                    v_from_y(v[:]).then_inc(s.v_set, 1)
                    norm(s, tl, tg).then_inc(s.shift_set, 1)
                if tl == HEADS and c == 4:
                    dve.wait_ge(s.side_hi_set, 2 * GROUPS + tg + 1)
                    cut_low(side_lo, p_turn[:], side_hi, F_UP).then_inc(s.side_lo_set, 1)
                if tl == HEADS and c == 6:
                    dve.wait_ge(s.h_done, tg + 1)
                    dve.wait_ge(s.fhi_set, 3 * GROUPS + tg)
                    dve.wait_ge(s.flo_set, 3 * GROUPS + tg)
                    nc.vector.scalar_tensor_tensor(out=w[:, :, 0:P], in0=p_h[:], scalar=DOWN, in1=bias(b2a_s),
                                                   op0=ALU.mult, op1=ALU.add).then_inc(s.w_part, 1)
                    dve.wait_ge(s.w_part, tg + 1)
                    nc.vector.tensor_tensor(w[:, :, 0:P], w[:, :, 0:P],
                                            rows(r_norm, tg).unsqueeze(2).to_broadcast([P, GT, P]),
                                            ALU.mult).then_inc(s.w_set, 1)
                    cut_w(s, tl, tg)
                if tl == NORM and c == 2:
                    nc.vector.tensor_tensor(none[:], rows(adj_r, tg), rows(r_norm, tg), ALU.add).then_inc(s.extra_set, 1)
                    dve.wait_ge(s.extra_set, 2 * tg + 1)
                    nc.vector.tensor_tensor(none[:], none[:], rows(r_norm, tg), ALU.mult).then_inc(s.extra_set, 1)
                    dve.wait_ge(s.extra_set, 2 * tg + 2)
                    dve.wait_ge(s.x_new, 2 * GROUPS + tg)
                    for j in range(GT):
                        last = nc.vector.scalar_tensor_tensor(out=v[:, j, :], in0=b2b_s[:], scalar=none[:, j:j + 1],
                                                              in1=xs[:, bass.ds(tg * GT + j, 1), :].rearrange("p a b -> p (a b)"),
                                                              op0=ALU.mult, op1=ALU.add)
                    last.then_inc(s.pre_set, 1)
                if tl == NORM and c == 3:
                    dve.wait_ge(s.y_done, n + 1)
                    dve.wait_ge(s.pre_set, GROUPS + tg + 1)
                    v_from_scaled_y(r_norm_down, tg).then_inc(s.v_set, 1)
                    norm(s, tl, tg, lambda j: xs[:, bass.ds(tg * GT + j, 1), :].rearrange("p a b -> p (a b)")).then_inc(s.x_new, 1)
                    dve.wait_ge(s.x_new, 2 * GROUPS + tg + 1)
                    dve.wait_ge(s.fhi_set, 4 * GROUPS + tg)
                    dve.wait_ge(s.flo_set, 4 * GROUPS + tg)
                    nc.vector.tensor_tensor(w[:], rows(xs, tg), rows(r_last, tg).unsqueeze(2).to_broadcast([P, GT, D]),
                                            ALU.mult).then_inc(s.w_set, 1)
                if tl == NORM and c == 4:
                    dve.wait_ge(s.w_set, GROUPS + tg + 1)
                    cut_w(s, tl, tg)
                if tl == LAST and c == 2:
                    dve.wait_ge(s.x_new, 3 * GROUPS)
                    free(dve, s.out_set, tg)
                    nc.vector.tensor_tensor(v[:], rows(xs, tg), bias(b3_s), ALU.add).then_inc(s.pre_set, 1)
                if tl == LAST and c == 3:
                    dve.wait_ge(s.y_done, n + 1)
                    dve.wait_ge(s.pre_set, 2 * GROUPS + tg + 1)
                    v_from_scaled_y(r_last_down, tg).then_inc(s.v_set, 1)
                    dve.wait_ge(s.x_kept, GROUPS)
                    free(dve, s.out_written, 16 * tg)
                    norm(s, tl, tg, lambda j: u[:, j, :]).then_inc(s.out_set, 1)

            def group(s, l, g):
                for c in range(CHUNKS):
                    if l == CONV1 and is_first(g):
                        first_features(s, c)
                    if s is by_mask and l == CONV1 and c == 0:
                        dve.wait_ge(values_in, 16 * (g + 1))
                    if l == HEADS and c < 2:
                        tail(s, *tail_of(l, g), c)
                    stream(s, l, g, c)
                    if l != HEADS or c >= 2:
                        tail(s, *tail_of(l, g), c)
                    if s is by_mask and l == CONV1 and is_second(g):
                        cut_weights(c)

            def last(s, tl, tg):
                for c in range(CHUNKS):
                    tail(s, tl, tg, c)

            def decided():
                dve.wait_ge(surplus_added, GROUPS)
                nc.vector.tensor_scalar(zero_rows[:], value_rows[:], 0.0, None, ALU.is_equal).then_inc(odd_step, 1)
                dve.wait_ge(odd_step, 1)
                nc.vector.tensor_reduce(odd_ones[:, 0:1], surplus[:], AXX, ALU.add)
                nc.vector.tensor_reduce(odd_ones[:, 1:2], zero_rows[:], AXX, ALU.add).then_inc(odd_counted, 1)
                dve.wait_ge(odd_summed, 1)
                nc.vector.tensor_reduce(odd_sum[0:1, :], p_h[0:1, 0, 0:2], AXX, ALU.add).then_inc(odd_step, 1)
                dve.wait_ge(odd_step, 2)
                nc.vector.tensor_scalar(one_value[:], odd_sum[0:1, :], 0.0, None, ALU.is_equal).then_inc(one_value_set, 1)

            run(dve, group, last, decided, nothing)


_INS = ["x", "xT", "adjT", "diag", "diagT", "w1", "w2", "wh", "w2a", "w2b", "w3", "b1", "b2", "bh", "b2a", "b2b", "b3"]


def kernel(x, adj, L0_gnn_W1, L0_gnn_b1, L0_gnn_W2, L0_gnn_b2, L1_gnn_W, L1_gnn_b, L2_gnn_W1, L2_gnn_b1,
           L2_gnn_W2, L2_gnn_b2, L3_gnn_W, L3_gnn_b):
    import numpy as np
    import concourse.bacc as bacc
    from concourse.bass_utils import run_bass_kernel_spmd

    x, adj = np.asarray(x), np.asarray(adj)
    heads = np.asarray(L1_gnn_W)
    data = {
        "x": x,
        "xT": x.T,
        "adjT": adj.reshape(GROUPS, GROUP, CHUNKS, CT, P).transpose(0, 2, 4, 3, 1).reshape(GROUPS, CHUNKS, P, CW),
        "diag": np.diagonal(adj),
        "diagT": np.diagonal(adj).reshape(TILES, P).T,
        "w1": np.asarray(L0_gnn_W1),
        "w2": np.asarray(L0_gnn_W2),
        "wh": heads.transpose(1, 0, 2).reshape(D, D),
        "w2a": np.asarray(L2_gnn_W1).T,
        "w2b": np.asarray(L2_gnn_W2).T,
        "w3": np.asarray(L3_gnn_W).T,
        "b1": np.asarray(L0_gnn_b1),
        "b2": np.asarray(L0_gnn_b2),
        "bh": np.asarray(L1_gnn_b).reshape(D),
        "b2a": np.asarray(L2_gnn_b1),
        "b2b": np.asarray(L2_gnn_b2),
        "b3": np.asarray(L3_gnn_b),
    }
    nc = bacc.Bacc("TRN2", target_bir_lowering=False, num_devices=1)
    arrays, args = {}, []
    for name in _INS:
        a = np.ascontiguousarray(data[name])
        arrays[f"in_{name}"] = a
        args.append(nc.dram_tensor(f"in_{name}", a.shape, mybir.dt.from_np(a.dtype), kind="ExternalInput").ap())
    args.append(nc.dram_tensor("out", (N, D), F32, kind="ExternalOutput").ap())
    gnn_kernel(nc, *args)
    r = run_bass_kernel_spmd(nc, [arrays], core_ids=[0])
    return r.results[0]["out"]
```
